# Optimizing a Trainium2 kernel written in Bass

```python
import numpy as np
import jax
import jax.numpy as jnp

def _softmax(x, axis=-1):
    return jax.nn.softmax(x, axis=axis)

def _gelu(x):
    return jax.nn.gelu(x, approximate=True)

def _silu(x):
    return jax.nn.silu(x)

def _sigmoid(x):
    return jax.nn.sigmoid(x)

def _layernorm(x, axis=-1, eps=1e-05):
    m = jnp.mean(x, axis=axis, keepdims=True)
    v = jnp.var(x, axis=axis, keepdims=True)
    return (x - m) / jnp.sqrt(v + eps)

def _scatter_add(tgt, idx, src, axis=0):
    return tgt.at[idx].add(src)

def _segment_sum(src, seg, n):
    return jax.ops.segment_sum(src, seg, n)
kernel_name = 'mk_cond_resid_d2_seqx_r2_80887e'

def setup_inputs(seed: int=0):
    np.random.seed(seed)
    _w = jnp.asarray

    def _rec_inputs():
        import jax
        import jax.numpy as jnp
        _rk = jax.random.key(seed)
        x = 0.5 + 0.2887 * jax.random.normal(jax.random.fold_in(_rk, 1), (2, 2048, 512), jnp.float32)
        _lenS = 2048 - jax.random.randint(jax.random.fold_in(_rk, 7), (2,), 0, max(1, 2048 // 4) + 1, jnp.int32)
        _lenS2 = 2048 - jax.random.randint(jax.random.fold_in(_rk, 8), (2,), 0, max(1, 2048 // 4) + 1, jnp.int32)
        condB_zX = jax.random.uniform(jax.random.fold_in(_rk, 11), (2,), jnp.float32, 0.0, 0.983423)
        condB_zY = jax.random.uniform(jax.random.fold_in(_rk, 12), (2,), jnp.float32, 0.0, 0.979075)
        condB_zR = jax.random.uniform(jax.random.fold_in(_rk, 13), (2,), jnp.float32, 0.0, 0.9968)
        itok_B_0_2 = jax.random.randint(jax.random.fold_in(_rk, 14), (2,), 0, 3, jnp.int32)
        return (x, condB_zX, condB_zY, condB_zR, itok_B_0_2)
    x, condB_zX, condB_zY, condB_zR, itok_B_0_2 = _rec_inputs()

    def _L0_cond_setup():
        import jax, jax.numpy as jnp
        import numpy as np
        key = jax.random.key(seed)
        k1, k2, k3, k4 = jax.random.split(key, 4)
        B, H, W = (64, 512, 512)
        return {'y': jax.random.uniform(k1, (B, H, W), dtype=jnp.float32), 'zX': jax.random.uniform(k2, (B, 1), dtype=jnp.float32), 'zY': jax.random.uniform(k3, (B, 1), dtype=jnp.float32), 'zR': jax.random.uniform(k4, (B, 1), dtype=jnp.float32), 'dx': 1, 'dy': 1}
    _L0_cond_all = _L0_cond_setup()
    _L0_cond_in = {k: v for k, v in _L0_cond_all.items() if k in ()}
    del _L0_cond_all

    def _L1_cond_setup():
        import jax, jax.numpy as jnp
        import numpy as np
        NEG_INF = -1e+30
        key = jax.random.key(seed)
        k1, k2, k3, k4, k5 = jax.random.split(key, 5)
        B, S, D, A = (16, 512, 512, 128)
        hidden = jax.random.normal(k1, (B, S, D), dtype=jnp.float32)
        W1 = jax.random.normal(k2, (D, A), dtype=jnp.float32) / np.sqrt(D)
        b1 = jax.random.normal(k3, (A,), dtype=jnp.float32) * 0.01
        v = jax.random.normal(k4, (A,), dtype=jnp.float32) / np.sqrt(A)
        prompt_type_ids = jax.random.randint(k5, (B,), 0, 3, dtype=jnp.int32)
        return {'hidden': hidden, 'W1': W1, 'b1': b1, 'v': v, 'prompt_type_ids': prompt_type_ids}
    _L1_cond_all = _L1_cond_setup()
    _L1_cond_in = {k: v for k, v in _L1_cond_all.items() if k in ('W1', 'b1', 'v')}
    del _L1_cond_all
    return {'x': x, 'condB_zX': condB_zX, 'condB_zY': condB_zY, 'condB_zR': condB_zR, 'itok_B_0_2': itok_B_0_2, 'L1_cond_W1': _L1_cond_in['W1'], 'L1_cond_b1': _L1_cond_in['b1'], 'L1_cond_v': _L1_cond_in['v']}

def reference(x, condB_zX, condB_zY, condB_zR, itok_B_0_2, L1_cond_W1, L1_cond_b1, L1_cond_v):
    import jax
    import jax.numpy as jnp

    def _L0_cond_ref(y, zX, zY, zR, dx, dy):
        import jax, jax.numpy as jnp
        import numpy as np
        yp_x = jnp.pad(y, ((0, 0), (0, 0), (1, 1)), mode='reflect')
        lap_x = (yp_x[:, :, :-2] - 2.0 * y + yp_x[:, :, 2:]) / (dx * dx)
        yp_y = jnp.pad(y, ((0, 0), (1, 1), (0, 0)), mode='reflect')
        lap_y = (yp_y[:, :-2, :] - 2.0 * y + yp_y[:, 2:, :]) / (dy * dy)
        du_dt = zX[:, :, None] * lap_x + zY[:, :, None] * lap_y + zR[:, :, None] * y * (1.0 - y)
        return du_dt

    def _L1_cond_ref(hidden, W1, b1, v, prompt_type_ids):
        import jax, jax.numpy as jnp
        import numpy as np
        NEG_INF = -1e+30
        B, S, D = hidden.shape
        attn_in = jnp.tanh(jnp.einsum('bsd,da->bsa', hidden, W1) + b1)
        scores = jnp.einsum('bsa,a->bs', attn_in, v)
        idx = jnp.arange(S)
        j = idx[:, None]
        l = idx[None, :]
        prefix_m = l <= j
        postfix_m = l >= j
        cloze_m = l != j
        pt = prompt_type_ids[:, None, None]
        mask = jnp.where(pt == 0, prefix_m[None], jnp.where(pt == 1, postfix_m[None], cloze_m[None]))
        masked_scores = jnp.where(mask, scores[:, None, :], NEG_INF)
        p = jax.nn.softmax(masked_scores, axis=-1)
        cnt = jnp.sum(mask, axis=-1).astype(hidden.dtype)
        pooled = jnp.einsum('bjl,bld->bjd', p, hidden) / cnt[..., None]
        return pooled
    x = x + _L0_cond_ref(x, condB_zX[:, None], condB_zY[:, None], condB_zR[:, None], 1, 1)
    x = x + _L1_cond_ref(x, L1_cond_W1, L1_cond_b1, L1_cond_v, itok_B_0_2)
    return x

_drawn_inputs = setup_inputs


def setup_inputs(seed=0):
    import zlib

    import numpy as np

    out = dict(_drawn_inputs(seed))
    spreads = {}
    factors = {}
    for name, (base, spread) in spreads.items():
        noise = np.random.default_rng([zlib.crc32(name.encode()), seed]).standard_normal(out[name].shape)
        drawn = base * np.exp(spread * noise) if base else spread * noise
        out[name] = jnp.asarray(drawn.astype(out[name].dtype))
    for name, factor in factors.items():
        out[name] = (out[name] * factor).astype(out[name].dtype)
    return out
```

```python
from contextlib import ExitStack

import concourse.bass as bass
from concourse import mybir

NB = 2
S = 2048
D = 512
A = 128
P = 128
NBLK = S // P
GB = 4
NGRP = NBLK // GB
TOT = NB * NBLK
DC = D // P
COPIES = P // NBLK
BIG = 1.0e30
CLAMP = 80.0
XS = 3
OS = 4

T_PART = {"hi": (0, 4, 6), "mid": (1, 5, 7), "lo": (2,)}

T_LAG = 2
W_LAG = 6
S_LAG = 8
CHAIN = 4 * (NGRP - 1) + S_LAG
B_LAG = 32
SLOTS = TOT + B_LAG


def build(nc, x, zX, zY, zR, itok, W1, b1, v, out):
    f32, bf16, i32 = mybir.dt.float32, mybir.dt.bfloat16, mybir.dt.int32
    ALU, ACT, AX = mybir.AluOpType, mybir.ActivationFunctionType, mybir.AxisListType

    ctx = ExitStack()
    with ctx:
        def sb(name, shape, dt=f32):
            return ctx.enter_context(nc.sbuf_tensor(name, shape, dt))

        def pb(name):
            return ctx.enter_context(nc.psum_tensor(name, [P, 512], f32))

        def sem(name):
            return ctx.enter_context(nc.semaphore(name))

        xin = sb("xin", [P, XS, GB, D + 2])
        x1 = sb("x1", [P, TOT, D])
        lr = sb("lr", [P, 2, GB, D])
        sq = sb("sq", [P, GB, D])
        x1T = sb("x1T", [P, 2, DC, GB * P])
        hT = sb("hT", [A, 2, GB * P])
        Pm = sb("Pm", [P, NB, NBLK, P])
        Wf = sb("Wf", [P, S])
        Wst = sb("Wst", [P, NB, S], bf16)
        Tf = sb("Tf", [P, D + 1])
        Th = sb("Th", [P, D + 1], bf16)
        Tm = sb("Tm", [P, D + 1], bf16)
        Tl = sb("Tl", [P, D + 1], bf16)
        Tst = sb("Tst", [P, NB, D + 2], bf16)
        TTr = sb("TTr", [P, DC, COPIES, NBLK])
        outs = sb("outs", [P, OS, D])

        halo = sb("halo", [96, NB, D])
        haloh = sb("haloh", [96, NB, D], bf16)
        halost = sb("halost", [96, NB, D], bf16)
        hsel = sb("hsel", [96, NBLK, P], bf16)
        ident = sb("ident", [P, P])
        offd = sb("offd", [P, P])
        tri = sb("tri", [P, NB, P])
        upper = sb("upper", [P, P])
        lower = sb("lower", [P, P])
        noteq = sb("noteq", [P, P])
        own = sb("own", [P, NB, P])
        W1s = sb("W1s", [P, DC, A])
        b1s = sb("b1s", [A, 1])
        vs = sb("vs", [A, 1])
        ones = sb("ones", [P, 1])
        one16 = sb("one16", [NBLK, P], bf16)
        eyeb = sb("eyeb", [NBLK, NBLK], bf16)
        repb = sb("repb", [NBLK, COPIES, NBLK], bf16)
        earlier = sb("earlier", [NBLK, NBLK], bf16)
        later = sb("later", [NBLK, NBLK], bf16)
        penF = sb("penF", [NBLK, NBLK])
        penB = sb("penB", [NBLK, NBLK])
        partrow = sb("partrow", [1, 3, P])
        part = sb("part", [P, 3])
        perm2 = sb("perm2", [P, 2, NBLK])
        permit = sb("permit", [P, NB, NBLK])
        permtmp = sb("permtmp", [P, NB, NBLK])
        posi = sb("posi", [P, NBLK], i32)
        pos = sb("pos", [P, NBLK])
        rpos = sb("rpos", [P, NBLK])
        cnt = sb("cnt", [P, NB, NBLK])
        z = sb("z", [P, 3, NB])
        ti = sb("ti", [P, NB], i32)
        tf = sb("tf", [P, NB])
        t = sb("t", [P, 3, NB])
        pen = sb("pen", [P, 3, NB])
        nt = sb("nt", [P, 2, NB])
        nzR = sb("nzR", [P, NB])
        cdia = sb("cdia", [P, NB])

        ssb = sb("ssb", [P, NB, NBLK])
        S16 = sb("S16", [NBLK, P])
        M16 = sb("M16", [NBLK, 1])
        Mb = sb("Mb", [NBLK, 1], bf16)
        Dm = sb("Dm", [NBLK, NBLK], bf16)
        Mr = sb("Mr", [P, NBLK + 1])
        earg = sb("earg", [P, NBLK])
        e = sb("e", [P, NBLK])
        erep = sb("erep", [P, COPIES, NBLK])
        RF = sb("RF", [NBLK, NBLK])
        RB = sb("RB", [NBLK, NBLK])
        Fb = sb("Fb", [NBLK, P + 1])
        Bb = sb("Bb", [NBLK, P + 1])
        m16 = sb("m16", [NBLK, P])
        mb = sb("mb", [NBLK, P], bf16)
        dc = sb("dc", [P, NB, NBLK])
        r = sb("r", [P, NB, NBLK])

        big = [pb(f"big{k}") for k in range(3)]
        tps = [pb(f"tps{k}") for k in range(2)]
        hps = pb("hps")
        sps = pb("sps")
        cps = pb("cps")

        s_x = [sem(f"s_x_slot{k}") for k in range(XS)]
        s_halo = sem("s_halo"); s_w1 = sem("s_w1"); s_small = sem("s_small")
        s_pool = sem("s_pool")
        s_pad = sem("s_pad"); s_lr = sem("s_lr"); s_sq = sem("s_sq")
        s_tri = sem("s_tri"); s_sel = sem("s_sel"); s_hst = sem("s_hst"); s_own = sem("s_own")
        s_cA = sem("s_cA"); s_cAp = sem("s_cAp")
        s_ps = sem("s_ps"); s_lin = sem("s_lin"); s_x1 = sem("s_x1")
        s_tp = sem("s_tp"); s_xT = sem("s_xT"); s_h = sem("s_h"); s_hT = sem("s_hT"); s_s = sem("s_s")
        s_dve = sem("s_dve")
        s_ssb = sem("s_ssb"); s_sT = sem("s_sT"); s_M = sem("s_M"); s_Mr = sem("s_Mr")
        s_ea = sem("s_ea"); s_e = sem("s_e"); s_er = sem("s_er"); s_TT = sem("s_TT")
        s_TTr = sem("s_TTr"); s_Trep = sem("s_Trep"); s_Tf = sem("s_Tf"); s_Tst = sem("s_Tst")
        s_m = sem("s_m"); s_mr = sem("s_mr"); s_mrc = sem("s_mrc")
        s_pa = sem("s_pa"); s_pe = sem("s_pe"); s_P = sem("s_P")
        s_wa = sem("s_wa"); s_we = sem("s_we"); s_wm = sem("s_wm"); s_W = sem("s_W")
        s_den = sem("s_den"); s_r = sem("s_r")
        s_psB = sem("s_psB"); s_o = sem("s_o"); s_st = [sem(f"s_store{k}") for k in range(OS)]

        block = ctx.enter_context(nc.Block())

        def ring_user(k):
            return big[k % 3]

        fills = []
        for i in range(SLOTS):
            if i < TOT:
                fills.append(("A", i))
            if i >= B_LAG:
                fills.append(("B", i - B_LAG))
        fill_of = {f: k for k, f in enumerate(fills)}

        def free_bank(pe, k):
            if k >= 3:
                kind, i = fills[k - 3]
                pe.wait_ge(s_lin if kind == "A" else s_o, i + 1)

        @block.sync
        def _(sp):
            for g in range(TOT // GB):
                if g >= XS:
                    sp.wait_ge(s_lr, g - XS + 1)
                    sp.wait_ge(s_sq, GB * (g - XS + 1))
                    sp.wait_ge(s_ps, GB * (g - XS + 1))
                n, q = divmod(g, NGRP)
                src = x[n, q * GB * P:(q + 1) * GB * P, :].rearrange("(k p) d -> p k d", p=P)
                sp.dma_start(xin[:, g % XS, :, 1:D + 1], src).then_inc(s_x[g % XS], 16)
                if g == 0:
                    sp.dma_start(W1s[:, :, :], W1.rearrange("(c p) a -> p c a", p=P)).then_inc(s_w1, 16)
            for j in range(TOT):
                n, q = divmod(j, NBLK)
                sp.wait_ge(s_o, j + 1)
                sp.dma_start(out[n, q * P:(q + 1) * P, :], outs[:, j % OS, :]).then_inc(s_st[j % OS], 16)
            for k in range(OS):
                sp.wait_ge(s_st[k], 16 * (TOT // OS))

        @block.scalar
        def _(act):
            for k, zz in enumerate((zX, zY, zR)):
                act.dma_start(z[:, k, :], zz.rearrange("(a n) -> a n", a=1).to_broadcast([P, NB])).then_inc(s_small, 16)
            act.dma_start(ti[:, :], itok.rearrange("(a n) -> a n", a=1).to_broadcast([P, NB])).then_inc(s_small, 16)
            for q in range(3):
                for n in range(NB):
                    base = 32 * q
                    act.dma_start(halo[base:base + 1, n, :], x[n, 1:2, :]).then_inc(s_halo, 16)
                    act.dma_start(halo[base + 1:base + 16, n, :], x[n, P - 1:S - 1:P, :]).then_inc(s_halo, 16)
                    act.dma_start(halo[base + 16:base + 31, n, :], x[n, P:S:P, :]).then_inc(s_halo, 16)
                    act.dma_start(halo[base + 31:base + 32, n, :], x[n, S - 2:S - 1, :]).then_inc(s_halo, 16)
            act.dma_start(b1s[:, :], b1.rearrange("(p a) -> p a", a=1)).then_inc(s_w1, 16)
            act.dma_start(vs[:, :], v.rearrange("(p a) -> p a", a=1)).then_inc(s_w1, 16)

            def square(i):
                g, k = divmod(i, GB)
                act.wait_ge(s_x[g % XS], 16 * (g // XS + 1))
                if i >= GB:
                    act.wait_ge(s_x1, i - GB + 1)
                nc.scalar.activation(sq[:, k, :], xin[:, g % XS, k, 1:D + 1], ACT.Square).then_inc(s_sq, 1)

            def evac_T(i):
                g = i // GB
                act.wait_ge(s_tp, i + 1)
                if g >= 2:
                    act.wait_ge(s_h, g - 1)
                nc.scalar.activation(x1T[:, g % 2, :, (i % GB) * P:(i % GB + 1) * P],
                                     tps[i % 2][:, :].rearrange("p (c t) -> p c t", c=DC), ACT.Copy).then_inc(s_xT, 1)

            def tanh(g):
                act.wait_ge(s_h, g + 1)
                if g >= 2:
                    act.wait_ge(s_s, g - 1)
                nc.scalar.activation(hT[:, g % 2, :], hps[:, :], ACT.Tanh, bias=b1s[:, 0:1]).then_inc(s_hT, 1)

            def exp_e(n):
                act.wait_ge(s_ea, n + 1)
                if n >= 1:
                    act.wait_ge(s_TT, n)
                nc.scalar.activation(e[:, :], earg[:, :], ACT.Exp).then_inc(s_e, 1)

            def evac_m(n, g):
                act.wait_ge(s_mr, NGRP * n + g + 1)
                if n >= 1:
                    act.wait_ge(s_W, n)
                nc.scalar.activation(Wf[:, g * 512:(g + 1) * 512], cps[:, :], ACT.Copy).then_inc(s_mrc, 1)

            def exp_P(n, g):
                act.wait_ge(s_pa, NBLK * n + GB * (g + 1))
                w = Pm[:, n, GB * g:GB * (g + 1), :]
                nc.scalar.activation(w, w, ACT.Exp, scale=-1.0).then_inc(s_pe, 1)

            def exp_W(n):
                act.wait_ge(s_wa, n + 1)
                nc.scalar.activation(Wf[:, :], Wf[:, :], ACT.Exp, scale=-1.0).then_inc(s_we, 1)

            act.wait_ge(s_w1, 48)
            square(0)
            square(1)
            for i in range(SLOTS):
                if i + 2 < TOT:
                    square(i + 2)
                if T_LAG <= i < TOT + T_LAG:
                    evac_T(i - T_LAG)
                g, k = divmod(i - W_LAG, GB)
                if k == 0 and 0 <= g < TOT // GB:
                    tanh(g)
                for n in range(NB):
                    c = i - CHAIN - NBLK * n
                    if c == 2:
                        exp_e(n)
                    if 5 <= c < 5 + NGRP:
                        evac_m(n, c - 5)
                    if 6 <= c < 6 + NGRP:
                        exp_P(n, c - 6)
                    if c == 5 + NGRP:
                        exp_W(n)

        @block.gpsimd
        def _(pool):
            seq = [0]

            def link(ins):
                seq[0] += 1
                ins.then_inc(s_pool, 1)
                pool.wait_ge(s_pool, seq[0])

            def select(tile, pattern, base, cm, op=ALU.not_equal, fill=1.0):
                link(pool.affine_select(out=tile, in_=tile, compare_op=op, fill=fill, base=base,
                                        pattern=pattern, channel_multiplier=cm))

            def pad_lr(g):
                pool.wait_ge(s_x[g % XS], 16 * (g // XS + 1))
                t_ = xin[:, g % XS]
                pool.tensor_copy(t_[:, :, 0:1], t_[:, :, 2:3]).then_inc(s_pad, 1)
                pool.tensor_copy(t_[:, :, D + 1:D + 2], t_[:, :, D - 1:D]).then_inc(s_pad, 1)
                pool.wait_ge(s_pad, 2 * (g + 1))
                if g >= 2:
                    pool.wait_ge(s_x1, GB * (g - 1))
                pool.tensor_tensor(lr[:, g % 2, :, :], t_[:, :, 0:D], t_[:, :, 2:D + 2], ALU.add).then_inc(s_lr, 1)

            link(pool.memset(ident[:, :], 0.0))
            select(ident[:, :], [[-1, P]], 0, 1)
            link(pool.memset(offd[:, :], 0.0))
            select(offd[:, :], [[-1, P]], 1, 1)
            pool.affine_select(out=offd[:, :], in_=offd[:, :], compare_op=ALU.not_equal, fill=1.0, base=-1,
                               pattern=[[-1, P]], channel_multiplier=1).then_inc(s_cA, 1)
            link(pool.memset(hsel[:, :, :], 0.0))
            for q in range(3):
                h = hsel[32 * q:32 * q + 32, :, :].rearrange("r b m -> r (b m)")
                select(h, [[-1, NBLK * P]], 0, P)
                select(h, [[-1, NBLK * P]], P - 1 - NBLK * P, P)
            pool.nop().then_inc(s_sel, 1)
            pad_lr(0)
            pad_lr(1)
            link(pool.memset(upper[:, :], 1.0))
            select(upper[:, :], [[1, P]], 0, -1, ALU.is_ge, 0.0)
            link(pool.memset(lower[:, :], 1.0))
            select(lower[:, :], [[-1, P]], 0, 1, ALU.is_ge, 0.0)
            link(pool.memset(noteq[:, :], 1.0))
            select(noteq[:, :], [[-1, P]], 0, 1, ALU.not_equal, 0.0)
            link(pool.memset(ones[:, :], 1.0))
            link(pool.memset(one16[:, :], 1.0))
            link(pool.memset(eyeb[:, :], 0.0))
            select(eyeb[:, :], [[-1, NBLK]], 0, 1)
            link(pool.memset(repb[:, :, :], 0.0))
            select(repb[:, :, :], [[0, COPIES], [-1, NBLK]], 0, 1)
            link(pool.memset(earlier[:, :], 1.0))
            select(earlier[:, :], [[1, NBLK]], 0, -1, ALU.is_gt, 0.0)
            link(pool.memset(later[:, :], 1.0))
            select(later[:, :], [[-1, NBLK]], 0, 1, ALU.is_gt, 0.0)
            link(pool.memset(penF[:, :], 0.0))
            select(penF[:, :], [[-1, NBLK]], 0, 1, ALU.is_gt, -BIG)
            link(pool.memset(penB[:, :], 0.0))
            select(penB[:, :], [[1, NBLK]], 0, -1, ALU.is_gt, -BIG)
            link(pool.memset(partrow[:, :, :], 0.0))
            for k, name in enumerate(("hi", "mid", "lo")):
                for c in T_PART[name]:
                    link(pool.memset(partrow[0:1, k, c * NBLK:(c + 1) * NBLK], 1.0))
            link(pool.iota(posi[:, :], pattern=[[P, NBLK]], base=1, channel_multiplier=1))
            link(pool.tensor_copy(pos[:, :], posi[:, :]))
            pool.tensor_scalar(rpos[:, :], pos[:, :], -1.0, float(S + 1), ALU.mult, ALU.add).then_inc(s_cAp, 1)

            def mask_P(n, g):
                pool.wait_ge(s_pe, NGRP * n + g + 1)
                if n == 0 and g == 0:
                    pool.wait_ge(s_own, 1)
                w = Pm[:, n, GB * g:GB * (g + 1), :]
                o = own[:, n:n + 1, :].to_broadcast([P, GB, P])
                pool.tensor_tensor(w, w, o, ALU.mult).then_inc(s_P, 1)

            def mask_W(n):
                pool.wait_ge(s_we, n + 1)
                w = Wf[:, :].rearrange("p (b j) -> p b j", b=NBLK)
                pm = permit[:, n, :].rearrange("p (b o) -> p b o", o=1).to_broadcast([P, NBLK, P])
                pool.tensor_tensor(w, w, pm, ALU.mult).then_inc(s_wm, 1)

            for i in range(SLOTS):
                if i % GB == 1 and i // GB + 2 < TOT // GB:
                    pad_lr(i // GB + 2)
                for n in range(NB):
                    c = i - CHAIN - NBLK * n
                    if 6 <= c < 6 + NGRP:
                        mask_P(n, c - 6)
                    if c == 5 + NGRP:
                        mask_W(n)

        @block.vector
        def _(dve):
            seq = [0]

            def link(ins):
                seq[0] += 1
                ins.then_inc(s_dve, 1)
                dve.wait_ge(s_dve, seq[0])

            vec = nc.vector
            dve.wait_ge(s_small, 64)
            link(vec.tensor_tensor(cdia[:, :], z[:, 0, :], z[:, 1, :], ALU.add))
            link(vec.scalar_tensor_tensor(out=cdia[:, :], in0=cdia[:, :], scalar=-2.0, in1=z[:, 2, :], op0=ALU.mult, op1=ALU.add))
            link(vec.tensor_scalar(cdia[:, :], cdia[:, :], 1.0, None, ALU.add))
            link(vec.tensor_scalar(nzR[:, :], z[:, 2, :], -1.0, None, ALU.mult))
            dve.wait_ge(s_cA, 1)
            for n in range(NB):
                link(vec.tensor_scalar(tri[:, n, :], ident[:, :], cdia[:, n:n + 1], None, ALU.mult))
                vec.scalar_tensor_tensor(out=tri[:, n, :], in0=offd[:, :], scalar=z[:, 1, n:n + 1], in1=tri[:, n, :],
                                         op0=ALU.mult, op1=ALU.add).then_inc(s_tri, 1)
            dve.wait_ge(s_halo, 16 * 24)
            for n in range(NB):
                link(vec.tensor_scalar(halo[:, n, :], halo[:, n, :], z[0:96, 1, n:n + 1], None, ALU.mult))
            link(vec.tensor_copy(haloh[:, :, :], halo[:, :, :]))
            vec.tensor_copy(halost[0:32, :, :], haloh[0:32, :, :]).then_inc(s_hst, 1)
            link(vec.tensor_tensor(halo[:, :, :], halo[:, :, :], haloh[:, :, :], ALU.subtract))
            link(vec.tensor_copy(haloh[:, :, :], halo[:, :, :]))
            vec.tensor_copy(halost[32:64, :, :], haloh[32:64, :, :]).then_inc(s_hst, 1)
            link(vec.tensor_tensor(halo[64:96, :, :], halo[64:96, :, :], haloh[64:96, :, :], ALU.subtract))
            vec.tensor_copy(halost[64:96, :, :], halo[64:96, :, :]).then_inc(s_hst, 1)

            def flags():
                link(vec.tensor_copy(tf[:, :], ti[:, :]))
                link(vec.tensor_scalar(t[:, 0, :], tf[:, :], 0.0, None, ALU.is_equal))
                link(vec.tensor_scalar(t[:, 1, :], tf[:, :], 1.0, None, ALU.is_equal))
                link(vec.tensor_tensor(t[:, 2, :], t[:, 0, :], t[:, 1, :], ALU.add))
                link(vec.tensor_scalar(t[:, 2, :], t[:, 2, :], -1.0, 1.0, ALU.mult, ALU.add))
                link(vec.tensor_scalar(pen[:, :, :], t[:, :, :], BIG, -BIG, ALU.mult, ALU.add))
                link(vec.tensor_scalar(nt[:, :, :], t[:, 0:2, :], -1.0, 1.0, ALU.mult, ALU.add))
                dve.wait_ge(s_cAp, 1)
                for n in range(NB):
                    link(vec.tensor_scalar(own[:, n, :], upper[:, :], t[:, 0, n:n + 1], None, ALU.mult))
                    link(vec.scalar_tensor_tensor(out=own[:, n, :], in0=lower[:, :], scalar=t[:, 1, n:n + 1], in1=own[:, n, :],
                                                  op0=ALU.mult, op1=ALU.add))
                    link(vec.scalar_tensor_tensor(out=own[:, n, :], in0=noteq[:, :], scalar=t[:, 2, n:n + 1], in1=own[:, n, :],
                                                  op0=ALU.mult, op1=ALU.add))
                    link(vec.tensor_scalar(cnt[:, n, :], pos[:, :], t[:, 0, n:n + 1], None, ALU.mult))
                    link(vec.scalar_tensor_tensor(out=cnt[:, n, :], in0=rpos[:, :], scalar=t[:, 1, n:n + 1], in1=cnt[:, n, :],
                                                  op0=ALU.mult, op1=ALU.add))
                    link(vec.tensor_scalar(permtmp[:, n, 0:1], t[:, 2, n:n + 1], float(S - 1), None, ALU.mult))
                    link(vec.tensor_scalar(cnt[:, n, :], cnt[:, n, :], permtmp[:, n, 0:1], None, ALU.add))
                dve.wait_ge(s_cA, 2)
                link(vec.tensor_copy(perm2[:, :, :], cps[:, 0:2 * NBLK].rearrange("p (a b) -> p a b", a=2)))
                link(vec.tensor_copy(part[:, :], cps[:, 2 * NBLK:2 * NBLK + 3]))
                for n in range(NB):
                    link(vec.tensor_scalar(permtmp[:, n, :], perm2[:, 0, :], nt[:, 1, n:n + 1], None, ALU.mult))
                    ins = vec.scalar_tensor_tensor(out=permit[:, n, :], in0=perm2[:, 1, :], scalar=nt[:, 0, n:n + 1],
                                                   in1=permtmp[:, n, :], op0=ALU.mult, op1=ALU.add)
                    link(ins)
                vec.tensor_copy(tf[:, :], ti[:, :]).then_inc(s_own, 1)

            def stencil(i):
                g, k = divmod(i, GB)
                n = i // NBLK
                dve.wait_ge(s_ps, i + 1)
                dve.wait_ge(s_lr, g + 1)
                vec.scalar_tensor_tensor(out=lr[:, g % 2, k, :], in0=lr[:, g % 2, k, :], scalar=z[:, 0, n:n + 1],
                                         in1=ring_user(fill_of["A", i])[:, :], op0=ALU.mult, op1=ALU.add).then_inc(s_lin, 1)
                dve.wait_ge(s_sq, i + 1)
                dve.wait_ge(s_lin, i + 1)
                vec.scalar_tensor_tensor(out=x1[:, i, :], in0=sq[:, k, :], scalar=nzR[:, n:n + 1],
                                         in1=lr[:, g % 2, k, :], op0=ALU.mult, op1=ALU.add).then_inc(s_x1, 1)

            def scores(n):
                dve.wait_ge(s_s, NGRP * (n + 1))
                vec.tensor_copy(ssb[:, n, :], sps[:, 0:NBLK]).then_inc(s_ssb, 1)

            def block_max(n):
                dve.wait_ge(s_sT, n + 1)
                link(vec.tensor_copy(S16[:, :], cps[0:NBLK, 0:P]))
                link(vec.tensor_reduce(M16[:, :], S16[:, :], AX.X, ALU.max))
                link(vec.tensor_copy(Mb[:, :], M16[:, :]))
                link(vec.tensor_copy(M16[:, :], Mb[:, :]))
                vec.tensor_scalar(Dm[:, :], eyeb[:, :], M16[:, 0:1], None, ALU.mult).then_inc(s_M, 1)

            def row_max(n):
                dve.wait_ge(s_Mr, n + 1)
                link(vec.tensor_copy(Mr[:, :], cps[:, 0:NBLK + 1]))
                vec.tensor_tensor(earg[:, :], ssb[:, n, :], Mr[:, 0:NBLK], ALU.subtract).then_inc(s_ea, 1)
                link(vec.tensor_tensor(RF[:, :], Mr[0:NBLK, 0:NBLK], penF[:, :], ALU.add))
                link(vec.tensor_reduce(Fb[:, 0:1], RF[:, :], AX.X, ALU.max))
                link(vec.tensor_tensor(RB[:, :], Mr[0:NBLK, 0:NBLK], penB[:, :], ALU.add))
                link(vec.tensor_reduce(Bb[:, P:P + 1], RB[:, :], AX.X, ALU.max))
                link(vec.tensor_tensor_scan(Fb[:, 1:P + 1], S16[:, :], S16[:, :], Fb[:, 0:1], ALU.max, ALU.max))
                link(vec.tensor_tensor_scan(Bb[:, 0:P][:, ::-1], S16[:, ::-1], S16[:, ::-1], Bb[:, P:P + 1], ALU.max, ALU.max))
                link(vec.tensor_scalar(m16[:, :], Fb[:, 1:P + 1], pen[0:NBLK, 0, n:n + 1], None, ALU.add))
                for src, k in ((Fb[:, 0:P], 2), (Bb[:, 0:P], 1), (Bb[:, 1:P + 1], 2)):
                    link(vec.scalar_tensor_tensor(out=m16[:, :], in0=src, scalar=pen[0:NBLK, k, n:n + 1], in1=m16[:, :],
                                                  op0=ALU.add, op1=ALU.max))
                vec.tensor_copy(mb[:, :], m16[:, :]).then_inc(s_m, 1)

            def spread_e(n):
                dve.wait_ge(s_e, n + 1)
                vec.tensor_copy(erep[:, :, :], e[:, :].rearrange("p (o b) -> p o b", o=1).to_broadcast([P, COPIES, NBLK])).then_inc(s_er, 1)

            def spread_T(n):
                dve.wait_ge(s_TT, n + 1)
                link(vec.tensor_copy(Tf[:, D:D + 1], cps[:, DC * NBLK:DC * NBLK + 1]))
                src = cps[:, 0:DC * NBLK].rearrange("p (c o b) -> p c o b", c=DC, o=1).to_broadcast([P, DC, COPIES, NBLK])
                vec.tensor_copy(TTr[:, :, :, :], src).then_inc(s_TTr, 1)

            def split_T(n):
                dve.wait_ge(s_Trep, n + 1)
                vec.tensor_copy(Tf[:, 0:D], cps[:, :]).then_inc(s_Tf, 1)
                dve.wait_ge(s_Tf, n + 1)
                link(vec.tensor_copy(Th[:, :], Tf[:, :]))
                link(vec.tensor_tensor(Tf[:, :], Tf[:, :], Th[:, :], ALU.subtract))
                link(vec.tensor_copy(Tm[:, :], Tf[:, :]))
                link(vec.tensor_tensor(Tf[:, :], Tf[:, :], Tm[:, :], ALU.subtract))
                link(vec.tensor_scalar(Tl[:, :], Tf[:, :], part[:, 2:3], None, ALU.mult))
                link(vec.scalar_tensor_tensor(out=Tl[:, :], in0=Tm[:, :], scalar=part[:, 1:2], in1=Tl[:, :], op0=ALU.mult, op1=ALU.add))
                vec.scalar_tensor_tensor(out=Tst[:, n, 0:D + 1], in0=Th[:, :], scalar=part[:, 0:1], in1=Tl[:, :],
                                         op0=ALU.mult, op1=ALU.add).then_inc(s_Tst, 1)

            def arg_P(n, g):
                dve.wait_ge(s_mrc, NGRP * n + g + 1)
                for b in range(GB * g, GB * (g + 1)):
                    vec.tensor_scalar(Pm[:, n, b, :], Wf[:, b * P:(b + 1) * P], ssb[:, n, b:b + 1], -CLAMP,
                                      ALU.subtract, ALU.max).then_inc(s_pa, 1)

            def arg_W(n):
                dve.wait_ge(s_pa, NBLK * (n + 1))
                vec.tensor_scalar(Wf[:, :], Wf[:, :], Mr[:, NBLK:NBLK + 1], -CLAMP, ALU.subtract, ALU.max).then_inc(s_wa, 1)

            def split_W(n):
                dve.wait_ge(s_wm, n + 1)
                h = P // 2
                link(vec.tensor_copy(Wst[:, n, :], Wf[:, :]))
                link(vec.tensor_tensor(Wf[h:P, :], Wf[h:P, :], Wst[h:P, n, :], ALU.subtract))
                link(vec.tensor_copy(Wst[h:P, n, :], Wf[h:P, :]))
                q = 96
                vec.tensor_tensor(Wst[q:P, n, :], Wf[q:P, :], Wst[q:P, n, :], ALU.subtract).then_inc(s_W, 1)

            def norm(n):
                dve.wait_ge(s_den, n + 1)
                link(vec.tensor_tensor(dc[:, n, :], cps[:, 0:NBLK], cnt[:, n, :], ALU.mult))
                vec.reciprocal(r[:, n, :], dc[:, n, :]).then_inc(s_r, 1)

            def output(j):
                n, b = divmod(j, NBLK)
                dve.wait_ge(s_psB, j + 1)
                if b == 0:
                    dve.wait_ge(s_r, n + 1)
                if j >= OS:
                    dve.wait_ge(s_st[j % OS], 16 * (j // OS))
                vec.scalar_tensor_tensor(out=outs[:, j % OS, :], in0=ring_user(fill_of["B", j])[:, :], scalar=r[:, n, b:b + 1],
                                         in1=x1[:, j, :], op0=ALU.mult, op1=ALU.add).then_inc(s_o, 1)

            for i in range(SLOTS):
                if i < TOT:
                    stencil(i)
                if i == 3:
                    flags()
                if i >= B_LAG:
                    output(i - B_LAG)
                for n in range(NB):
                    c = i - CHAIN - NBLK * n
                    if c == 0:
                        scores(n)
                    if c == 1:
                        block_max(n)
                    if c == 2:
                        row_max(n)
                        spread_e(n)
                    if c == 3:
                        spread_T(n)
                    if c == 4:
                        split_T(n)
                    if 6 <= c < 6 + NGRP:
                        arg_P(n, c - 6)
                    if c == 5 + NGRP:
                        arg_W(n)
                        split_W(n)
                    if c == 11:
                        norm(n)

        @block.tensor
        def _(pe):
            mm = nc.tensor.matmul

            def tridiagonal(i):
                g, k = divmod(i, GB)
                n = i // NBLK
                ps = ring_user(fill_of["A", i])
                free_bank(pe, fill_of["A", i])
                pe.wait_ge(s_x[g % XS], 16 * (g // XS + 1))
                mm(ps[:, :], tri[:, n, :], xin[:, g % XS, k, 1:D + 1], start=True, stop=False)
                if i == 0:
                    pe.wait_ge(s_sel, 1)
                    pe.wait_ge(s_hst, 3)
                mm(ps[:, :], hsel[:, i % NBLK, :], halost[:, n, :], start=False, stop=True).then_inc(s_ps, 1)

            def transposes(i):
                pe.wait_ge(s_x1, i + 1)
                if i >= 2:
                    pe.wait_ge(s_xT, i - 1)
                for c in range(DC):
                    last = nc.tensor.transpose(tps[i % 2][:, c * P:(c + 1) * P], x1[:, i, c * P:(c + 1) * P], ident[:, :])
                last.then_inc(s_tp, 1)

            def w1_product(g):
                pe.wait_ge(s_xT, GB * (g + 1))
                if g >= 1:
                    pe.wait_ge(s_hT, g)
                if g == 0:
                    pe.wait_ge(s_w1, 48)
                for c in range(DC):
                    last = mm(hps[:, :], W1s[:, c, :], x1T[:, g % 2, c, :], start=(c == 0), stop=(c == DC - 1))
                last.then_inc(s_h, 1)

            def score(g):
                pe.wait_ge(s_hT, g + 1)
                if g % NGRP == 0 and g:
                    pe.wait_ge(s_ssb, g // NGRP)
                for k in range(GB):
                    b = (g % NGRP) * GB + k
                    last = mm(sps[:, b:b + 1], hT[:, g % 2, k * P:(k + 1) * P], vs[:, 0:1], start=True, stop=True)
                last.then_inc(s_s, 1)

            def chain(n, c):
                if c == 1:
                    pe.wait_ge(s_ssb, n + 1)
                    if n == 0:
                        pe.wait_ge(s_own, 1)
                    else:
                        pe.wait_ge(s_r, n)
                    nc.tensor.transpose(cps[0:NBLK, 0:P], ssb[:, n, :], ident[:, :]).then_inc(s_sT, 1)
                if c == 2:
                    pe.wait_ge(s_M, n + 1)
                    mm(cps[:, 0:NBLK], one16[:, :], Dm[:, :], start=True, stop=True)
                    mm(cps[:, NBLK:NBLK + 1], repb[:, :, :].rearrange("k c b -> k (c b)"), Mb[:, :], start=True, stop=True).then_inc(s_Mr, 1)
                if c == 3:
                    pe.wait_ge(s_er, n + 1)
                    pe.wait_ge(s_x1, NBLK * (n + 1))
                    for b in range(NBLK):
                        for k in range(DC):
                            mm(cps[:, k * NBLK + b:k * NBLK + b + 1], x1[:, n * NBLK + b, k * P:(k + 1) * P], e[:, b:b + 1],
                               start=True, stop=True)
                    mm(cps[:, DC * NBLK:DC * NBLK + 1], erep[:, :, :].rearrange("k c b -> k (c b)"), ones[:, :],
                       start=True, stop=True).then_inc(s_TT, 1)
                if c == 4:
                    pe.wait_ge(s_TTr, n + 1)
                    for k in range(DC):
                        last = nc.tensor.transpose(cps[:, k * P:(k + 1) * P], TTr[:, k, :, :].rearrange("p c b -> p (c b)"), ident[:, :])
                    last.then_inc(s_Trep, 1)
                if 5 <= c < 5 + NGRP:
                    g = c - 5
                    if g == 0:
                        pe.wait_ge(s_m, n + 1)
                        pe.wait_ge(s_Tf, n + 1)
                    else:
                        pe.wait_ge(s_mrc, NGRP * n + g)
                    for k in range(GB):
                        b = g * GB + k
                        last = mm(cps[:, k * P:(k + 1) * P], eyeb[:, b:b + 1].to_broadcast([NBLK, P]), mb[:, :],
                                  start=True, stop=True)
                    last.then_inc(s_mr, 1)
                if c == 11:
                    pe.wait_ge(s_mrc, NGRP * (n + 1))
                    pe.wait_ge(s_P, NGRP * (n + 1))
                    pe.wait_ge(s_Tst, n + 1)
                    pe.wait_ge(s_W, n + 1)
                    for b in range(NBLK):
                        mm(cps[:, b:b + 1], Pm[:, n, b, :], ones[:, :], start=True, stop=False)
                        last = mm(cps[:, b:b + 1], Wst[:, n, b * P:(b + 1) * P], Tst[:, n, D:D + 1], start=False, stop=True)
                    last.then_inc(s_den, 1)

            def pooled(j):
                n, b = divmod(j, NBLK)
                ps = ring_user(fill_of["B", j])
                free_bank(pe, fill_of["B", j])
                mm(ps[:, :], Pm[:, n, b, :], x1[:, j, :], start=True, stop=False)
                mm(ps[:, :], Wst[:, n, b * P:(b + 1) * P], Tst[:, n, 0:D], start=False, stop=True).then_inc(s_psB, 1)

            pe.wait_ge(s_tri, NB)
            for i in range(SLOTS):
                if i < TOT:
                    tridiagonal(i)
                if i >= B_LAG:
                    pooled(i - B_LAG)
                if T_LAG <= i < TOT + T_LAG:
                    transposes(i - T_LAG)
                if i == 3:
                    pe.wait_ge(s_cAp, 1)
                    rep = repb[:, :, :].rearrange("k c b -> k (c b)")
                    mm(cps[:, 0:NBLK], rep, earlier[:, :], start=True, stop=True)
                    mm(cps[:, NBLK:2 * NBLK], rep, later[:, :], start=True, stop=True)
                    for k in range(3):
                        last = mm(cps[:, 2 * NBLK + k:2 * NBLK + k + 1], partrow[0:1, k, :], ones[0:1, :], start=True, stop=True)
                    last.then_inc(s_cA, 1)
                g, k = divmod(i - W_LAG, GB)
                if k == 0 and 0 <= g < TOT // GB:
                    w1_product(g)
                g, k = divmod(i - S_LAG, GB)
                if k == 0 and 0 <= g < TOT // GB:
                    score(g)
                for n in range(NB):
                    chain(n, i - CHAIN - NBLK * n)


_INS = ["x", "condB_zX", "condB_zY", "condB_zR", "itok_B_0_2", "L1_cond_W1", "L1_cond_b1", "L1_cond_v"]


def kernel(**inputs):
    import numpy as np
    import concourse.bacc as bacc
    from concourse.bass_utils import run_bass_kernel_spmd

    nc = bacc.Bacc("TRN2", target_bir_lowering=False, num_devices=1)
    arrays, args = {}, []
    for name in _INS:
        a = np.ascontiguousarray(inputs[name])
        arrays[f"in_{name}"] = a
        args.append(nc.dram_tensor(f"in_{name}", a.shape, mybir.dt.from_np(a.dtype), kind="ExternalInput").ap())
    out = nc.dram_tensor("out", (NB, S, D), mybir.dt.float32, kind="ExternalOutput").ap()
    build(nc, *args, out)
    r = run_bass_kernel_spmd(nc, [arrays], core_ids=[0])
    return r.results[0]["out"]
```

```python
from contextlib import ExitStack

import concourse.bass as bass
from concourse import mybir

NB = 2
S = 2048
D = 512
A = 128
P = 128
GB = 4
T = GB * P
NBLK = S // P
NG = S // T
TOT = NB * NBLK
GROUPS = NB * NG
DC = D // P
BIG = 1.0e30
V_MAX = 20.0
CLAMP = 80.0
XS = 4
LS = 4
XP = 2
OS = 4
RS = 5
TAIL = GB * (GROUPS - 3)
LAG = 4


def build(nc, x, zX, zY, zR, itok, W1, b1, v, out):
    f32, i32 = mybir.dt.float32, mybir.dt.int32
    ALU, ACT = mybir.AluOpType, mybir.ActivationFunctionType

    ctx = ExitStack()
    with ctx:
        def sb(name, shape, dt=f32):
            return ctx.enter_context(nc.sbuf_tensor(name, shape, dt))

        def pb(name):
            return ctx.enter_context(nc.psum_tensor(name, [P, 512], f32))

        def sem(name):
            return ctx.enter_context(nc.semaphore(name))

        xin = sb("xin", [P, XS, 2, D])
        xs = sb("xs", [P, 2, 2, D + 2])
        lr = sb("lr", [P, 2, 2, D])
        loc = sb("loc", [P, LS, 2, D])
        x1T = sb("x1T", [P, RS, DC, T])
        G = sb("G", [P, RS, DC, T])
        hT = sb("hT", [A, T])
        srow = sb("srow", [P, S])
        outs = sb("outs", [P, OS, D])

        ident = sb("ident", [P, P])
        tri = sb("tri", [P, NB, P])
        bT = sb("bT", [P, DC, 2 * TOT])
        W1s = sb("W1s", [P, DC, A])
        b1s = sb("b1s", [A, 1])
        vs = sb("vs", [A, 1])
        vrep = sb("vrep", [A, P])
        z = sb("z", [P, 3, NB])
        ti = sb("ti", [P, NB], i32)
        allow = sb("allow", [P, 3, NB])
        pen = sb("pen", [P, 3, NB])
        cslope = sb("cslope", [P, NB])
        cbase = sb("cbase", [P, NB])
        nzR = sb("nzR", [P, NB])
        cdia = sb("cdia", [P, NB])

        L_r = sb("L_r", [P, T + 1])
        ab = sb("ab", [P, 2, T])
        one = sb("one", [P, 1])
        cnt = sb("cnt", [P, NBLK])
        fac = sb("fac", [P, TOT])
        pooled = sb("pooled", [P, 2, D])
        vabs = sb("vabs", [A, 1])
        fast = sb("fast", [P, NB])
        fasti = sb("fasti", [P, NB], i32)

        mF = sb("mF", [P, S + 1])
        mB = sb("mB", [P, S + 1])
        LF = sb("LF", [P, S + 1])
        LB = sb("LB", [P, S + 1])
        w3 = sb("w3", [P, 3, T])
        rden = sb("rden", [P, T])
        tf = rden[:, 0:NB]
        t = rden[:, 8:8 + 3 * NB].rearrange("p (k n) -> p k n", k=3)
        cnti = rden[:, 32:32 + NBLK].bitcast(i32)
        dec = sb("dec", [P, T])
        brow = dec[0:2 * TOT, :]
        wgt = sb("wgt", [P, T])
        offd = wgt[:, 0:P]
        back = L_r
        carry = sb("carry", [P, DC])

        xps = [pb(f"xps{k}") for k in range(XP)]
        xbk = [pb(f"xbk{k}") for k in range(2)]
        qbk = [pb(f"qbk{k}") for k in range(2)]
        hps = pb("hps")

        def x1_bank(j):
            return (xbk + xps)[j % 4] if j >= TAIL else xbk[j % 2]

        lps = pb("lps")

        s_x = [sem(f"s_x_slot{k}") for k in range(XS)]
        s_v1 = sem("s_v1"); s_fast = sem("s_fast"); s_cnt = sem("s_cnt"); s_L = sem("s_L"); s_Lc = sem("s_Lc"); s_fac = sem("s_fac")
        s_bkQ = sem("s_bkQ"); s_pl = sem("s_pl")
        s_small = sem("s_small"); s_ti = sem("s_ti"); s_brow = sem("s_brow"); s_w = sem("s_w")
        s_pool = sem("s_pool")
        s_con = sem("s_con")
        s_tri = sem("s_tri"); s_bt = sem("s_bt"); s_vrep = sem("s_vrep"); s_bT = sem("s_bT")
        s_xs = sem("s_xs"); s_pad = sem("s_pad"); s_lr = [sem("s_lr_even"), sem("s_lr_odd")]; s_sq = sem("s_sq"); s_loc = sem("s_loc")
        s_A = sem("s_A"); s_xT = sem("s_xT"); s_fix = sem("s_fix")
        s_h = sem("s_h"); s_hT = sem("s_hT"); s_s = sem("s_s"); s_srow = sem("s_srow")
        s_G = sem("s_G"); s_bkx = sem("s_bkx"); s_o = sem("s_o")
        s_store = [sem(f"s_store{k}") for k in range(OS)]
        s_dve = sem("s_dve")
        s_dp = [sem(f"s_dp{n}") for n in range(NB)]
        s_dg = [sem(f"s_dg{n}") for n in range(NB)]
        s_arg = [sem(f"s_arg{n}") for n in range(NB)]
        s_exp = [sem(f"s_exp{n}") for n in range(NB)]
        s_garg = [sem(f"s_garg{n}") for n in range(NB)]
        s_gexp = [sem(f"s_gexp{n}") for n in range(NB)]

        block = ctx.enter_context(nc.Block())

        def small(eng, k, zz):
            eng.dma_start(z[:, k, :], zz.rearrange("(a n) -> a n", a=1).to_broadcast([P, NB])).then_inc(s_small, 16)

        @block.sync
        def _(sp):
            def load(p):
                if p >= XS:
                    sp.wait_ge(s_sq, p - XS + 1)
                    sp.wait_ge(s_xs, p - XS + 1)
                    sp.wait_ge(s_A, 2 * (p - XS + 1))
                n, h = divmod(p, NBLK // 2)
                src = x[n, h * 2 * P:(h + 1) * 2 * P, :].rearrange("(k p) d -> p k d", p=P)
                sp.dma_start(xin[:, p % XS, :, :], src).then_inc(s_x[p % XS], 16)

            def store(j):
                if j < 0:
                    return
                n, b = divmod(j, NBLK)
                sp.wait_ge(s_o, j + 1)
                sp.dma_start(out[n, b * P:(b + 1) * P, :], outs[:, j % OS, :]).then_inc(s_store[j % OS], 16)

            load(0)
            small(sp, 1, zY)
            for p in range(1, XS):
                load(p)
            sp.dma_start(W1s[:, :, :], W1.rearrange("(c p) a -> p c a", p=P)).then_inc(s_w, 16)
            sp.dma_start(b1s[:, :], b1.rearrange("(p a) -> p a", a=1)).then_inc(s_w, 16)
            sp.dma_start(vs[:, :], v.rearrange("(p a) -> p a", a=1)).then_inc(s_w, 16)
            sp.dma_start(ti[:, :], itok.rearrange("(a n) -> a n", a=1).to_broadcast([P, NB])).then_inc(s_ti, 16)
            rows = x.rearrange("n s d -> (n s) d")
            sp.dma_start(brow[1:TOT, :], rows[P - 1:NB * S - 1:P, :]).then_inc(s_brow, 16)
            sp.dma_start(brow[TOT:2 * TOT - 1, :], rows[P:NB * S:P, :]).then_inc(s_brow, 16)
            sp.wait_ge(s_brow, 32)
            for n in range(NB):
                above, below = n * NBLK, TOT + (n + 1) * NBLK - 1
                sp.dma_start(brow[above:above + 1, :], x[n, 1:2, :]).then_inc(s_brow, 16)
                sp.dma_start(brow[below:below + 1, :], x[n, S - 2:S - 1, :]).then_inc(s_brow, 16)
            for k in range(1, GROUPS - 1):
                j = GB * (k - 1 - LAG)
                load(2 * k + 2)
                store(j)
                store(j + 1)
                load(2 * k + 3)
                store(j + 2)
                store(j + 3)
            for j in range(GB * (GROUPS - 2 - LAG), TOT):
                store(j)
            for k in range(OS):
                sp.wait_ge(s_store[k], 16 * (TOT // OS))

        def x_there(eng, p):
            eng.wait_ge(s_x[p % XS], 16 * (p // XS + 1))

        def add_shifted(eng, p):
            w = xs[:, p % 2]
            eng.tensor_tensor(lr[:, p % 2, :, :], w[:, :, 0:D], w[:, :, 2:D + 2], ALU.add).then_inc(s_lr[p % 2], 1)

        @block.scalar
        def _(act):
            small(act, 0, zX)
            small(act, 2, zR)
            act.wait_ge(s_small, 48)

            def scale_square(p):
                src = xin[:, p % XS, :, :]
                x_there(act, p)
                if p >= 2:
                    act.wait_ge(s_lr[p % 2], p // 2)
                nc.scalar.activation(xs[:, p % 2, :, 1:D + 1], src, ACT.Copy, scale=z[:, 0, p // (NBLK // 2):p // (NBLK // 2) + 1]).then_inc(s_xs, 1)
                if p >= LS:
                    act.wait_ge(s_A, 2 * (p - LS + 1))
                nc.scalar.activation(loc[:, p % LS, :, :], src, ACT.Square).then_inc(s_sq, 1)

            def keep_x1T(i):
                k, b = divmod(i, GB)
                act.wait_ge(s_A, i + 1)
                if k >= RS:
                    act.wait_ge(s_bkx, GB * (k - RS + 1))
                nc.scalar.activation(x1T[:, k % RS, :, b * P:(b + 1) * P],
                                     xps[i % XP][:, :].rearrange("p (c t) -> p c t", c=DC), ACT.Copy).then_inc(s_xT, 1)

            def tanh(k):
                act.wait_ge(s_h, k + 1)
                if k >= 1:
                    act.wait_ge(s_s, k)
                if k == 0:
                    act.wait_ge(s_w, 48)
                nc.scalar.activation(hT[:, :], hps[:, :], ACT.Tanh, bias=b1s[:, 0:1]).then_inc(s_hT, 1)

            def keep_scores(k):
                act.wait_ge(s_s, k + 1)
                if k >= NG:
                    act.wait_ge(s_G, DC * (k - NG + 1))
                nc.scalar.activation(srow[:, (k % NG) * T:(k % NG + 1) * T], hps[:, :], ACT.Copy).then_inc(s_srow, 1)

            def exp_general(k):
                n, g = divmod(k, NG)
                if g < NG - 1:
                    return
                step = [0]

                def exp(tile):
                    step[0] += 1
                    act.wait_ge(s_garg[n], step[0])
                    nc.scalar.activation(tile, tile, ACT.Exp).then_inc(s_gexp[n], 1)

                with act.If(short[n] == 0):
                    for _ in range(NG):
                        exp(ab[:, :, :])
                    for _ in range(NG):
                        exp(ab[:, :, :])
                        exp(w3[:, :, :])
                with act.Else():
                    act.nop()

            def exp_prefix(k):
                n, g = divmod(k, NG)
                with act.If(short[n] != 0):
                    act.wait_ge(s_arg[n], g + 1)
                    nc.scalar.activation(ab[:, k % 2, :], ab[:, k % 2, :], ACT.Exp).then_inc(s_exp[n], 1)
                with act.Else():
                    act.nop()

            def scale_pooled(j):
                act.wait_ge(s_bkQ, j + 1)
                if j % GB == 0:
                    act.wait_ge(s_fac, j // GB + 1)
                if j >= 2:
                    act.wait_ge(s_o, j - 1)
                nc.scalar.activation(pooled[:, j % 2, :], qbk[j % 2][:, :], ACT.Copy, scale=fac[:, j:j + 1]).then_inc(s_pl, 1)

            scale_square(0)
            scale_square(1)
            for k in range(GROUPS + 1):
                j = GB * (k - LAG)
                more = k < GROUPS
                if more:
                    keep_x1T(GB * k)
                if k + 1 < GROUPS:
                    scale_square(2 * k + 2)
                if more:
                    keep_x1T(GB * k + 1)
                if k + 1 < GROUPS:
                    scale_square(2 * k + 3)
                if k >= 1:
                    tanh(k - 1)
                if more:
                    keep_x1T(GB * k + 2)
                if k == 1:
                    act.wait_ge(s_fast, 1)
                    short = [act.value_load(fasti[0:1, n:n + 1]) for n in range(NB)]
                if k >= 1:
                    keep_scores(k - 1)
                    exp_general(k - 1)
                early = k >= LAG and k % NG != 0
                if early:
                    scale_pooled(j)
                if more and k < LAG:
                    keep_x1T(GB * k + 3)
                if k >= 1:
                    exp_prefix(k - 1)
                if k >= LAG and not early:
                    scale_pooled(j)
                if k >= LAG:
                    scale_pooled(j + 1)
                if more and k >= LAG:
                    keep_x1T(GB * k + 3)
                if k >= LAG:
                    scale_pooled(j + 2)
                    scale_pooled(j + 3)
            for j in range(GB * (GROUPS + 1 - LAG), TOT):
                scale_pooled(j)

        @block.gpsimd
        def _(pool):
            seq = [0]

            def link(ins):
                seq[0] += 1
                ins.then_inc(s_pool, 1)
                pool.wait_ge(s_pool, seq[0])

            def reflect(p):
                pool.wait_ge(s_xs, p + 1)
                w = xs[:, p % 2]
                pool.tensor_copy(w[:, :, 0:1], w[:, :, 2:3]).then_inc(s_pad, 1)
                pool.tensor_copy(w[:, :, D + 1:D + 2], w[:, :, D - 1:D]).then_inc(s_pad, 1)
                if p % 2 == 1:
                    pool.wait_ge(s_pad, 2 * (p + 1))
                    if p >= 2:
                        pool.wait_ge(s_loc, p - 1)
                    add_shifted(pool, p)

            link(pool.memset(ident[:, :], 0.0))
            link(pool.affine_select(out=ident[:, :], in_=ident[:, :], compare_op=ALU.not_equal, fill=1.0, base=0,
                                    pattern=[[-1, P]], channel_multiplier=1))
            link(pool.memset(offd, 0.0))
            for side in (1, -1):
                link(pool.affine_select(out=offd, in_=offd, compare_op=ALU.not_equal, fill=1.0, base=side,
                                        pattern=[[-1, P]], channel_multiplier=1))
            pool.nop().then_inc(s_con, 1)
            reflect(0)
            pool.memset(one[:, :], 1.0).then_inc(s_cnt, 1)
            link(pool.iota(cnti[:, :], pattern=[[P, NBLK]], base=1, channel_multiplier=1))
            pool.tensor_copy(cnt[:, :], cnti[:, :]).then_inc(s_cnt, 1)
            for p in range(1, TOT // 2):
                reflect(p)

        @block.vector
        def _(dve):
            vec = nc.vector

            def chain(s):
                seq = [0]

                def link(ins):
                    seq[0] += 1
                    ins.then_inc(s, 1)
                    dve.wait_ge(s, seq[0])
                return link

            link = chain(s_dve)
            plink = [chain(s) for s in s_dp]
            glink = [chain(s) for s in s_dg]

            dve.wait_ge(s_small, 48)
            link(vec.tensor_tensor(cdia[:, :], z[:, 0, :], z[:, 1, :], ALU.add))
            link(vec.scalar_tensor_tensor(out=cdia[:, :], in0=cdia[:, :], scalar=-2.0, in1=z[:, 2, :], op0=ALU.mult, op1=ALU.add))
            link(vec.tensor_scalar(cdia[:, :], cdia[:, :], 1.0, None, ALU.add))
            link(vec.tensor_scalar(nzR[:, :], z[:, 2, :], -1.0, None, ALU.mult))
            dve.wait_ge(s_con, 1)
            for n in range(NB):
                link(vec.tensor_scalar(tri[:, n, :], ident[:, :], cdia[:, n:n + 1], None, ALU.mult))
                vec.scalar_tensor_tensor(out=tri[:, n, :], in0=offd, scalar=z[:, 1, n:n + 1], in1=tri[:, n, :],
                                         op0=ALU.mult, op1=ALU.add).then_inc(s_tri, 1)
            dve.wait_ge(s_tri, NB)

            def left_right(p):
                dve.wait_ge(s_pad, 2 * (p + 1))
                if p >= 2:
                    dve.wait_ge(s_loc, p - 1)
                add_shifted(vec, p)

            def local(p):
                n = p // (NBLK // 2)
                dve.wait_ge(s_lr[p % 2], p // 2 + 1)
                dve.wait_ge(s_sq, p + 1)
                to = loc[:, p % LS, :, :]
                vec.scalar_tensor_tensor(out=to, in0=to, scalar=nzR[:, n:n + 1], in1=lr[:, p % 2, :, :],
                                         op0=ALU.mult, op1=ALU.add).then_inc(s_loc, 1)

            def borders(k):
                n, g = divmod(k, NG)
                dve.wait_ge(s_xT, GB * (k + 1))
                if k == 0:
                    dve.wait_ge(s_bT, NB)
                w = x1T[:, k % RS, :, :].rearrange("p c (b t) -> p c b t", b=GB)
                for side, col in ((0, 0), (TOT, P - 1)):
                    at = side + GB * k
                    edge = w[:, :, :, col:col + 1].rearrange("p c b t -> p c (b t)")
                    vec.tensor_tensor(edge, edge, bT[:, :, at:at + GB], ALU.add).then_inc(s_fix, 1)

            def constants():
                dve.wait_ge(s_w, 48)
                vec.tensor_scalar(vrep[:, :], ident[:, :], 0.0, vs[:, 0:1], ALU.mult, ALU.add).then_inc(s_vrep, 1)
                vec.scalar_tensor_tensor(out=vabs[:, :], in0=vs[:, :], scalar=-1.0, in1=vs[:, :], op0=ALU.mult, op1=ALU.max).then_inc(s_vrep, 1)
                dve.wait_ge(s_bt, 1)
                border = lps[:, 0:DC * 2 * TOT].rearrange("p (c r) -> p c r", c=2 * DC)
                scaled = bT.rearrange("p c (s r) -> p (c s) r", s=2)
                for n in range(NB):
                    rows = slice(NBLK * n, NBLK * (n + 1))
                    vec.tensor_scalar(scaled[:, :, rows], border[:, :, rows], z[:, 1, n:n + 1], None, ALU.mult).then_inc(s_bT, 1)

            def flags():
                dve.wait_ge(s_ti, 16)
                dve.wait_ge(s_cnt, 2)
                link(vec.tensor_copy(tf[:, :], ti[:, :]))
                link(vec.tensor_scalar(t[:, 0, :], tf[:, :], 0.0, None, ALU.is_equal))
                link(vec.tensor_scalar(t[:, 1, :], tf[:, :], 1.0, None, ALU.is_equal))
                link(vec.tensor_tensor(t[:, 2, :], t[:, 0, :], t[:, 1, :], ALU.add))
                link(vec.tensor_scalar(t[:, 2, :], t[:, 2, :], -1.0, 1.0, ALU.mult, ALU.add))
                for k, flag in enumerate((1, 0, 2)):
                    link(vec.tensor_scalar(allow[:, k, :], t[:, flag, :], -1.0, 1.0, ALU.mult, ALU.add))
                link(vec.tensor_scalar(pen[:, :, :], allow[:, :, :], BIG, -BIG, ALU.mult, ALU.add))
                link(vec.tensor_tensor(cslope[:, :], t[:, 0, :], t[:, 1, :], ALU.subtract))
                link(vec.tensor_scalar(cbase[:, :], t[:, 1, :], float(S + 1), None, ALU.mult))
                link(vec.scalar_tensor_tensor(out=cbase[:, :], in0=t[:, 2, :], scalar=float(S - 1), in1=cbase[:, :],
                                              op0=ALU.mult, op1=ALU.add))
                dve.wait_ge(s_v1, 1)
                link(vec.tensor_scalar(fast[:, :], t[:, 0, :], 0.0, None, ALU.mult))
                link(vec.tensor_scalar(fast[:, :], fast[:, :], lps[:, 511:512], V_MAX, ALU.add, ALU.is_le))
                link(vec.tensor_tensor(fast[:, :], fast[:, :], t[:, 0, :], ALU.mult))
                vec.tensor_copy(fasti[:, :], fast[:, :]).then_inc(s_fast, 1)
                dve.wait_ge(s_fast, 1)

            def slot_free(k):
                if k >= RS:
                    dve.wait_ge(s_bkQ, GB * (k - RS + 1))

            def over_chunks(row):
                return row.rearrange("p (o t) -> p o t", o=1).to_broadcast([P, DC, T])

            def prefix_rho(k):
                n, g = divmod(k, NG)
                lk = plink[n]
                o = g * T
                dve.wait_ge(s_srow, k + 1)
                rho = ab[:, k % 2, :]
                if g == 0:
                    lk(vec.memset(rho[:, 0:1], 0.0))
                    vec.tensor_tensor(rho[:, 1:T], srow[:, 0:T - 1], srow[:, 1:T], ALU.subtract).then_inc(s_arg[n], 1)
                else:
                    vec.tensor_tensor(rho, srow[:, o - 1:o + T - 1], srow[:, o:o + T], ALU.subtract).then_inc(s_arg[n], 1)

            def prefix_L(k):
                n, g = divmod(k, NG)
                lk = plink[n]
                dve.wait_ge(s_exp[n], g + 1)
                if k >= 1:
                    dve.wait_ge(s_Lc, k)
                if g == 0:
                    dve.wait_ge(s_cnt, 2)
                    lk(vec.memset(L_r[:, 0:1], 0.0))
                else:
                    lk(vec.tensor_copy(L_r[:, 0:1], L_r[:, T:T + 1]))
                vec.tensor_tensor_scan(L_r[:, 1:T + 1], ab[:, k % 2, :], one[:, 0:1].to_broadcast([P, T]), L_r[:, 0:1],
                                       ALU.mult, ALU.add).then_inc(s_L, 1)

            def prefix_scan(k):
                n, g = divmod(k, NG)
                prefix_L(k)
                slot_free(k)
                dve.wait_ge(s_fix, 2 * (k + 1))
                for c in range(DC):
                    start = 0.0 if g == 0 else G[:, (k - 1) % RS, c, T - 1:T]
                    vec.tensor_tensor_scan(G[:, k % RS, c, :], ab[:, k % 2, :], x1T[:, k % RS, c, :], start,
                                           ALU.mult, ALU.add).then_inc(s_G, 1)
                dve.wait_ge(s_L, k + 1)
                dve.wait_ge(s_G, DC * (k + 1))

            def prefix_factor(k):
                n, g = divmod(k, NG)
                lk = plink[n]
                f = fac[:, GB * k:GB * (k + 1)]
                dve.wait_ge(s_Lc, k + 1)
                lk(vec.tensor_tensor(f, lps[:, 0:GB], cnt[:, GB * g:GB * (g + 1)], ALU.mult))
                vec.reciprocal(f, f).then_inc(s_fac, 1)
                dve.wait_ge(s_fac, k + 1)

            def general(k):
                n = k // NG
                lk = glink[n]
                step = [0]

                def exp(ins):
                    step[0] += 1
                    ins.then_inc(s_garg[n], 1)
                    dve.wait_ge(s_gexp[n], step[0])

                dve.wait_ge(s_srow, k + 1)
                dve.wait_ge(s_cnt, 2)
                dve.wait_ge(s_fix, 2 * (k + 1))
                dve.wait_ge(s_Lc, k)
                slot_free(k)
                for col, val in ((mF[:, 0:1], -BIG), (mB[:, S:S + 1], -BIG), (LF[:, 0:1], 0.0), (LB[:, S:S + 1], 0.0)):
                    lk(vec.memset(col, val))
                unit = one[:, 0:1].to_broadcast([P, T])
                lk(vec.tensor_tensor_scan(mF[:, 1:S + 1], srow[:, :], srow[:, :], mF[:, 0:1], ALU.max, ALU.max))
                lk(vec.tensor_tensor_scan(mB[:, 0:S][:, ::-1], srow[:, ::-1], srow[:, ::-1], mB[:, S:S + 1], ALU.max, ALU.max))
                for g in range(NG):
                    o, slot = g * T, (NG * n + g) % RS
                    lk(vec.tensor_tensor(ab[:, 0, :], mF[:, o:o + T], mF[:, o + 1:o + T + 1], ALU.subtract))
                    exp(vec.tensor_tensor(ab[:, 1, :], srow[:, o:o + T], mF[:, o + 1:o + T + 1], ALU.subtract))
                    lk(vec.tensor_tensor_scan(LF[:, o + 1:o + T + 1], ab[:, 0, :], ab[:, 1, :], LF[:, o:o + 1], ALU.mult, ALU.add))
                    lk(vec.tensor_tensor(G[:, slot, :, :], x1T[:, slot, :, :], over_chunks(ab[:, 1, :]), ALU.mult))
                    for c in range(DC):
                        row = G[:, slot, c, :]
                        start = 0.0 if g == 0 else G[:, (NG * n + g - 1) % RS, c, T - 1:T]
                        lk(vec.tensor_tensor_scan(row, ab[:, 0, :], row, start, ALU.mult, ALU.add))
                for g in reversed(range(NG)):
                    o, slot = g * T, (NG * n + g) % RS
                    lk(vec.tensor_tensor(ab[:, 0, :], mB[:, o + 1:o + T + 1], mB[:, o:o + T], ALU.subtract))
                    exp(vec.tensor_tensor(ab[:, 1, :], srow[:, o:o + T], mB[:, o:o + T], ALU.subtract))
                    lk(vec.tensor_tensor_scan(LB[:, o:o + T][:, ::-1], ab[:, 0, ::-1], ab[:, 1, ::-1], LB[:, o + T:o + T + 1],
                                              ALU.mult, ALU.add))
                    src = (mF[:, o:o + T], mB[:, o + 1:o + T + 1], srow[:, o:o + T])
                    lk(vec.tensor_scalar(rden[:, :], src[0], pen[:, 0, n:n + 1], None, ALU.add))
                    for q in (1, 2):
                        lk(vec.scalar_tensor_tensor(out=rden[:, :], in0=src[q], scalar=pen[:, q, n:n + 1], in1=rden[:, :],
                                                    op0=ALU.add, op1=ALU.max))
                    for q in range(3):
                        lk(vec.tensor_tensor(w3[:, q, :], src[q], rden[:, :], ALU.subtract))
                    exp(vec.tensor_scalar(w3[:, :, :], w3[:, :, :], CLAMP, None, ALU.min))
                    for q in range(3):
                        lk(vec.tensor_scalar(w3[:, q, :], w3[:, q, :], allow[:, q, n:n + 1], None, ALU.mult))
                    lk(vec.tensor_tensor(dec[:, :], w3[:, 0, :], LF[:, o:o + T], ALU.mult))
                    lk(vec.tensor_tensor(wgt[:, :], w3[:, 1, :], LB[:, o + 1:o + T + 1], ALU.mult))
                    lk(vec.tensor_tensor(dec[:, :], dec[:, :], wgt[:, :], ALU.add))
                    lk(vec.tensor_tensor(dec[:, :], dec[:, :], w3[:, 2, :], ALU.add))
                    lk(vec.tensor_tensor_scan(rden[:, :], unit, unit, float(o), ALU.mult, ALU.add))
                    lk(vec.tensor_scalar(wgt[:, :], rden[:, :], cslope[:, n:n + 1], cbase[:, n:n + 1], ALU.mult, ALU.add))
                    lk(vec.tensor_tensor(dec[:, :], dec[:, :], wgt[:, :], ALU.mult))
                    lk(vec.reciprocal(rden[:, :], dec[:, :]))
                    for q in range(3):
                        lk(vec.tensor_tensor(w3[:, q, :], w3[:, q, :], rden[:, :], ALU.mult))
                    for c in range(DC):
                        row, x1row = G[:, slot, c, :], x1T[:, slot, c, :]
                        if g == NG - 1:
                            lk(vec.memset(back[:, T:T + 1], 0.0))
                        else:
                            lk(vec.tensor_copy(back[:, T:T + 1], carry[:, c:c + 1]))
                        lk(vec.tensor_tensor(back[:, 0:T], x1row, ab[:, 1, :], ALU.mult))
                        lk(vec.tensor_tensor_scan(back[:, 0:T][:, ::-1], ab[:, 0, ::-1], back[:, 0:T][:, ::-1], back[:, T:T + 1],
                                                  ALU.mult, ALU.add))
                        lk(vec.tensor_copy(carry[:, c:c + 1], back[:, 0:1]))
                        lk(vec.tensor_tensor(wgt[:, 1:T], w3[:, 0, 1:T], row[:, 0:T - 1], ALU.mult))
                        if g == 0:
                            lk(vec.memset(wgt[:, 0:1], 0.0))
                        else:
                            before = G[:, (NG * n + g - 1) % RS, c, T - 1:T]
                            lk(vec.tensor_tensor(wgt[:, 0:1], w3[:, 0, 0:1], before, ALU.mult))
                        lk(vec.tensor_tensor(dec[:, :], w3[:, 1, :], back[:, 1:T + 1], ALU.mult))
                        lk(vec.tensor_tensor(row, w3[:, 2, :], x1row, ALU.mult))
                        lk(vec.tensor_tensor(row, row, wgt[:, :], ALU.add))
                        lk(vec.tensor_tensor(row, row, dec[:, :], ALU.add))
                vec.memset(carry[:, 0:1], 0.0).then_inc(s_G, NG * DC)
                dve.wait_ge(s_G, DC * (k + 1))

            def branch(*steps):
                n = steps[0][0] // NG
                same = [step for step in steps if step[0] // NG == n]
                with dve.If(short[n] != 0):
                    for k, short_path, _ in same:
                        short_path(k)
                with dve.Else():
                    for k, _, other in same:
                        other(k)
                if len(same) < len(steps):
                    branch(*steps[len(same):])

            def no_L(k):
                if k >= 1:
                    dve.wait_ge(s_Lc, k)
                vec.memset(L_r[0:1, :], 1.0).then_inc(s_L, 1)
                dve.wait_ge(s_L, k + 1)

            def scan_general(k):
                if k % NG == NG - 1:
                    general(k)
                else:
                    dve.nop()

            def one_factor(k):
                dve.wait_ge(s_Lc, k + 1)
                vec.memset(fac[:, GB * k:GB * (k + 1)], 1.0).then_inc(s_fac, 1)

            def output(j):
                dve.wait_ge(s_pl, j + 1)
                dve.wait_ge(s_bkx, j + 1)
                if j >= OS:
                    dve.wait_ge(s_store[j % OS], 16 * (j // OS))
                vec.tensor_tensor(outs[:, j % OS, :], pooled[:, j % 2, :], x1_bank(j)[:, :], ALU.add).then_inc(s_o, 1)

            left_right(0)
            local(0)
            local(1)
            constants()
            for k in range(GROUPS + 1):
                j = GB * (k - LAG)
                if k >= 1:
                    borders(k - 1)
                if k >= 2:
                    branch((k - 2, prefix_scan, no_L))
                if k + 1 < GROUPS:
                    left_right(2 * k + 2)
                    local(2 * k + 2)
                    if k == 0:
                        local(3)
                        flags()
                        short = [dve.value_load(fasti[0:1, n:n + 1]) for n in range(NB)]
                if k >= 2:
                    branch((k - 2, prefix_factor, one_factor), (k - 1, prefix_rho, scan_general))
                elif k == 1:
                    branch((0, prefix_rho, scan_general))
                if k >= LAG:
                    output(j)
                    output(j + 1)
                if 1 <= k < GROUPS - 1:
                    local(2 * k + 3)
                if k >= LAG:
                    output(j + 2)
                    output(j + 3)
            for j in range(GB * (GROUPS + 1 - LAG), TOT):
                if j == GB * (GROUPS + 1 - LAG) + 1:
                    branch((GROUPS - 1, prefix_scan, no_L))
                if j == TOT - GB:
                    branch((GROUPS - 1, prefix_factor, one_factor))
                output(j)

        @block.tensor
        def _(pe):
            mm = nc.tensor.matmul

            def stencil(i):
                n = i // NBLK
                p = i // 2
                ps = xps[i % XP]
                x_there(pe, p)
                pe.wait_ge(s_loc, p + 1)
                if i >= XP:
                    pe.wait_ge(s_xT, i - XP + 1)
                for c in range(DC):
                    to = ps[:, c * P:(c + 1) * P]
                    mm(to, xin[:, p % XS, i % 2, c * P:(c + 1) * P], tri[:, n, :], start=True, stop=False)
                    last = mm(to, loc[:, p % LS, i % 2, c * P:(c + 1) * P], ident[:, :], is_transpose=True, start=False, stop=True)
                last.then_inc(s_A, 1)

            def w1_product(k):
                pe.wait_ge(s_fix, 2 * (k + 1))
                if k >= 1:
                    pe.wait_ge(s_srow, k)
                else:
                    pe.wait_ge(s_w, 48)
                for c in range(DC):
                    last = mm(hps[:, :], W1s[:, c, :], x1T[:, k % RS, c, :], start=(c == 0), stop=(c == DC - 1))
                last.then_inc(s_h, 1)

            def scores(k):
                pe.wait_ge(s_hT, k + 1)
                mm(hps[:, :], vrep[:, :], hT[:, :], start=True, stop=True).then_inc(s_s, 1)

            def turn_L(k):
                pe.wait_ge(s_L, k + 1)
                if k >= 1:
                    pe.wait_ge(s_fac, k)
                else:
                    pe.wait_ge(s_fast, 1)
                for b in range(GB):
                    last = nc.tensor.transpose(lps[:, b:b + 1], L_r[0:1, 1 + b * P:1 + (b + 1) * P], ident[0:1, 0:1])
                last.then_inc(s_Lc, 1)

            def back_x1(j):
                k, b = divmod(j, GB)
                if TAIL <= j < TAIL + 4:
                    pe.wait_ge(s_xT, TOT)
                    pe.wait_ge(s_o, TAIL)
                elif j >= TAIL:
                    pe.wait_ge(s_o, j - 3)
                elif j >= 2:
                    pe.wait_ge(s_o, j - 1)
                for c in range(DC):
                    last = nc.tensor.transpose(x1_bank(j)[:, c * P:(c + 1) * P], x1T[:, k % RS, c, b * P:(b + 1) * P], ident[:, :])
                last.then_inc(s_bkx, 1)

            def back_Q(j):
                k, b = divmod(j, GB)
                pe.wait_ge(s_G, DC * (k + 1))
                if j >= 2:
                    pe.wait_ge(s_pl, j - 1)
                for c in range(DC):
                    last = nc.tensor.transpose(qbk[j % 2][:, c * P:(c + 1) * P], G[:, k % RS, c, b * P:(b + 1) * P], ident[:, :])
                last.then_inc(s_bkQ, 1)

            pe.wait_ge(s_con, 1)
            pe.wait_ge(s_tri, NB)
            for k in range(GROUPS + 1):
                j = GB * (k - LAG)
                more = k < GROUPS
                if more:
                    stencil(GB * k)
                    if k == 0:
                        pe.wait_ge(s_brow, 32 * (NB + 1))
                        for c in range(DC):
                            last = nc.tensor.transpose(lps[:, c * 2 * TOT:(c + 1) * 2 * TOT], brow[:, c * P:(c + 1) * P],
                                                       ident[0:2 * TOT, 0:2 * TOT])
                        last.then_inc(s_bt, 1)
                    stencil(GB * k + 1)
                if k >= LAG:
                    back_x1(j)
                if k >= 1:
                    w1_product(k - 1)
                if k >= LAG:
                    back_x1(j + 1)
                if k >= 2:
                    turn_L(k - 2)
                if more:
                    stencil(GB * k + 2)
                    if k == 0:
                        pe.wait_ge(s_vrep, 2)
                        pe.wait_ge(s_cnt, 2)
                        pe.wait_ge(s_bT, NB)
                        mm(lps[:, 511:512], one[:, 0:1].to_broadcast([A, P]), vabs[:, :], start=True, stop=True).then_inc(s_v1, 1)
                if k >= 1:
                    scores(k - 1)
                if k >= LAG:
                    back_Q(j)
                    back_Q(j + 1)
                if more:
                    stencil(GB * k + 3)
                if k >= LAG:
                    back_x1(j + 2)
                    back_Q(j + 2)
                    back_x1(j + 3)
                    back_Q(j + 3)
            for j in range(GB * (GROUPS + 1 - LAG), TOT):
                if j == TOT - GB:
                    turn_L(GROUPS - 1)
                back_Q(j)
                back_x1(j)


_INS = ["x", "condB_zX", "condB_zY", "condB_zR", "itok_B_0_2", "L1_cond_W1", "L1_cond_b1", "L1_cond_v"]


def kernel(**inputs):
    import numpy as np
    import concourse.bacc as bacc
    from concourse.bass_utils import run_bass_kernel_spmd

    nc = bacc.Bacc("TRN2", target_bir_lowering=False, num_devices=1)
    arrays, args = {}, []
    for name in _INS:
        a = np.ascontiguousarray(inputs[name])
        arrays[f"in_{name}"] = a
        args.append(nc.dram_tensor(f"in_{name}", a.shape, mybir.dt.from_np(a.dtype), kind="ExternalInput").ap())
    out = nc.dram_tensor("out", (NB, S, D), mybir.dt.float32, kind="ExternalOutput").ap()
    build(nc, *args, out)
    r = run_bass_kernel_spmd(nc, [arrays], core_ids=[0])
    return r.results[0]["out"]
```

```python
from contextlib import ExitStack

import concourse.bass as bass
from concourse import mybir

NB = 2
S = 2048
D = 512
A = 128
P = 128
GB = 4
T = GB * P
NBLK = S // P
NG = S // T
TOT = NB * NBLK
GROUPS = NB * NG
DC = D // P
BIG = 1.0e30
V_MAX = 20.0
CLAMP = 80.0
XS = 4
LS = 4
XP = 2
OS = 6
RS = 5
LAG = 4
WARM = 17
TAIL = GB * (GROUPS - LAG)


def build(nc, x, zX, zY, zR, itok, W1, b1, v, out):
    f32, i32 = mybir.dt.float32, mybir.dt.int32
    ALU, ACT = mybir.AluOpType, mybir.ActivationFunctionType

    ctx = ExitStack()
    with ctx:
        def sb(name, shape, dt=f32):
            return ctx.enter_context(nc.sbuf_tensor(name, shape, dt))

        def pb(name):
            return ctx.enter_context(nc.psum_tensor(name, [P, 512], f32))

        def sem(name):
            return ctx.enter_context(nc.semaphore(name))

        xin = sb("xin", [P, XS, 2, D])
        xs = sb("xs", [P, 2, 2, D + 2])
        lr = sb("lr", [P, 2, 2, D])
        loc = sb("loc", [P, LS, 2, D])
        x1T = sb("x1T", [P, RS, DC, T])
        G = sb("G", [P, RS, DC, T])
        hT = sb("hT", [A, T])
        srow = sb("srow", [P, S])
        outs = sb("outs", [P, OS, D])

        ident = sb("ident", [P, P])
        tri = sb("tri", [P, NB, P])
        bT = sb("bT", [P, DC, 2 * TOT])
        W1s = sb("W1s", [P, DC, A])
        b1s = sb("b1s", [A, 1])
        vs = sb("vs", [A, 1])
        vrep = sb("vrep", [A, P])
        z = sb("z", [P, 3, NB])
        ti = sb("ti", [P, NB], i32)
        allow = sb("allow", [P, 3, NB])
        pen = sb("pen", [P, 3, NB])
        cslope = sb("cslope", [P, NB])
        cbase = sb("cbase", [P, NB])
        nzR = sb("nzR", [P, NB])
        cdia = sb("cdia", [P, NB])

        L_r = sb("L_r", [P, T + 1])
        ab = sb("ab", [P, 2, T])
        one = sb("one", [P, 1])
        spare = sb("spare", [P, 1])
        cnt = sb("cnt", [P, NBLK])
        fac = sb("fac", [P, TOT])
        vabs = sb("vabs", [A, 1])
        fast = sb("fast", [P, NB])
        fasti = sb("fasti", [P, NB], i32)

        mF = sb("mF", [P, S + 1])
        mB = sb("mB", [P, S + 1])
        LF = sb("LF", [P, S + 1])
        LB = sb("LB", [P, S + 1])
        w3 = sb("w3", [P, 3, T])
        rden = sb("rden", [P, T])
        tf = rden[:, 0:NB]
        t = rden[:, 8:8 + 3 * NB].rearrange("p (k n) -> p k n", k=3)
        cnti = rden[:, 32:32 + NBLK].bitcast(i32)
        dec = sb("dec", [P, T])
        brow = dec[0:2 * TOT, :]
        wgt = sb("wgt", [P, T])
        offd = wgt[:, 0:P]
        back = L_r
        carry = sb("carry", [P, DC])

        xps = [pb(f"xps{k}") for k in range(XP)]
        xbk = [pb(f"xbk{k}") for k in range(2)]
        qbk = [pb(f"qbk{k}") for k in range(2)]
        hps = pb("hps")

        def x1_bank(j):
            return (xbk + xps)[j % 4] if j >= TAIL else xbk[j % 2]

        def q_bank(j):
            return (qbk + [hps])[(j - TAIL) % 3] if j >= TAIL else qbk[j % 2]

        lps = pb("lps")

        s_x = [sem(f"s_x_slot{k}") for k in range(XS)]
        s_small = sem("s_small")
        s_ti = sem("s_ti")
        s_w = sem("s_w")
        s_brow = sem("s_brow")
        s_one = sem("s_one")
        s_con = sem("s_con")
        s_cnt = sem("s_cnt")
        s_pool = sem("s_pool")
        s_tri = sem("s_tri")
        s_vrep = sem("s_vrep")
        s_v1 = sem("s_v1")
        s_fast = sem("s_fast")
        s_bt = sem("s_bt")
        s_bT = sem("s_bT")
        s_xs = sem("s_xs")
        s_pad = sem("s_pad")
        s_sq = sem("s_sq")
        s_lr = [sem("s_lr_even"), sem("s_lr_odd")]
        s_loc = sem("s_loc")
        s_A = sem("s_A")
        s_xT = sem("s_xT")
        s_fix = sem("s_fix")
        s_h = sem("s_h")
        s_hT = sem("s_hT")
        s_s = sem("s_s")
        s_srow = sem("s_srow")
        s_L = sem("s_L")
        s_Lc = sem("s_Lc")
        s_fac = sem("s_fac")
        s_G = sem("s_G")
        s_bkQ = sem("s_bkQ")
        s_bkx = sem("s_bkx")
        s_pl = sem("s_pl")
        s_o = sem("s_o")
        s_store = [sem(f"s_store{k}") for k in range(OS)]
        s_dve = sem("s_dve")
        s_dp = [sem(f"s_dp{n}") for n in range(NB)]
        s_dg = [sem(f"s_dg{n}") for n in range(NB)]
        s_arg = [sem(f"s_arg{n}") for n in range(NB)]
        s_exp = [sem(f"s_exp{n}") for n in range(NB)]
        s_garg = [sem(f"s_garg{n}") for n in range(NB)]
        s_gexp = [sem(f"s_gexp{n}") for n in range(NB)]

        block = ctx.enter_context(nc.Block())

        def small(eng, k, zz):
            eng.dma_start(z[:, k, :], zz.rearrange("(a n) -> a n", a=1).to_broadcast([P, NB])).then_inc(s_small, 16)

        @block.sync
        def _(sp):
            def load(p):
                if p >= XS:
                    sp.wait_ge(s_sq, p - XS + 1)
                    sp.wait_ge(s_xs, p - XS + 1)
                    sp.wait_ge(s_A, 2 * (p - XS + 1))
                n, h = divmod(p, NBLK // 2)
                src = x[n, h * 2 * P:(h + 1) * 2 * P, :].rearrange("(k p) d -> p k d", p=P)
                sp.dma_start(xin[:, p % XS, :, :], src).then_inc(s_x[p % XS], 16)

            def store(j):
                if j < 0:
                    return
                n, b = divmod(j, NBLK)
                sp.wait_ge(s_o, j + 1)
                sp.dma_start(out[n, b * P:(b + 1) * P, :], outs[:, j % OS, :]).then_inc(s_store[j % OS], 16)

            load(0)
            small(sp, 1, zY)
            load(1)
            rows = x.rearrange("n s d -> (n s) d")
            sp.dma_start(brow[1:TOT, :], rows[P - 1:NB * S - 1:P, :]).then_inc(s_brow, 16)
            sp.dma_start(brow[TOT:2 * TOT - 1, :], rows[P:NB * S:P, :]).then_inc(s_brow, 16)
            load(2)
            load(3)
            sp.dma_start(W1s[:, :, :], W1.rearrange("(c p) a -> p c a", p=P)).then_inc(s_w, 16)
            sp.dma_start(b1s[:, :], b1.rearrange("(p a) -> p a", a=1)).then_inc(s_w, 16)
            sp.dma_start(vs[:, :], v.rearrange("(p a) -> p a", a=1)).then_inc(s_w, 16)
            sp.dma_start(ti[:, :], itok.rearrange("(a n) -> a n", a=1).to_broadcast([P, NB])).then_inc(s_ti, 16)
            sp.wait_ge(s_brow, 32)
            for n in range(NB):
                above, below = n * NBLK, TOT + (n + 1) * NBLK - 1
                sp.dma_start(brow[above:above + 1, :], x[n, 1:2, :]).then_inc(s_brow, 16)
                sp.dma_start(brow[below:below + 1, :], x[n, S - 2:S - 1, :]).then_inc(s_brow, 16)
            for k in range(1, GROUPS - 1):
                j = GB * (k - 1 - LAG)
                load(2 * k + 2)
                store(j)
                store(j + 1)
                load(2 * k + 3)
                store(j + 2)
                store(j + 3)
            for j in range(GB * (GROUPS - 2 - LAG), TOT):
                store(j)
            for k in range(OS):
                sp.wait_ge(s_store[k], 16 * len(range(k, TOT, OS)))

        def x_there(eng, p):
            eng.wait_ge(s_x[p % XS], 16 * (p // XS + 1))

        def pool_adds(p):
            return p % 2 == 1 and p >= 4

        def add_shifted(eng, p):
            w = xs[:, p % 2]
            eng.tensor_tensor(lr[:, p % 2, :, :], w[:, :, 0:D], w[:, :, 2:D + 2], ALU.add).then_inc(s_lr[p % 2], 1)

        @block.scalar
        def _(act):
            small(act, 0, zX)
            small(act, 2, zR)
            act.wait_ge(s_one, 1)
            nc.scalar.activation(spare[:, :], one[:, :], ACT.Exp)
            act.wait_ge(s_small, 48)

            def scale(p):
                n = p // (NBLK // 2)
                x_there(act, p)
                if p >= 2:
                    act.wait_ge(s_lr[p % 2], p // 2)
                nc.scalar.activation(xs[:, p % 2, :, 1:D + 1], xin[:, p % XS, :, :], ACT.Copy, scale=z[:, 0, n:n + 1]).then_inc(s_xs, 1)

            def square(p):
                if p >= LS:
                    act.wait_ge(s_A, 2 * (p - LS + 1))
                nc.scalar.activation(loc[:, p % LS, :, :], xin[:, p % XS, :, :], ACT.Square).then_inc(s_sq, 1)

            def scale_square(p):
                scale(p)
                square(p)

            def keep_x1T(i):
                k, b = divmod(i, GB)
                act.wait_ge(s_A, i + 1)
                if k >= RS:
                    act.wait_ge(s_bkx, GB * (k - RS + 1))
                nc.scalar.activation(x1T[:, k % RS, :, b * P:(b + 1) * P],
                                     xps[i % XP][:, :].rearrange("p (c t) -> p c t", c=DC), ACT.Copy).then_inc(s_xT, 1)

            def tanh(k):
                act.wait_ge(s_h, k + 1)
                if k >= 1:
                    act.wait_ge(s_s, k)
                if k == 0:
                    act.wait_ge(s_w, 48)
                nc.scalar.activation(hT[:, :], hps[:, :], ACT.Tanh, bias=b1s[:, 0:1]).then_inc(s_hT, 1)

            def keep_scores(k):
                act.wait_ge(s_s, k + 1)
                if k >= NG:
                    act.wait_ge(s_G, DC * (k - NG + 1))
                nc.scalar.activation(srow[:, (k % NG) * T:(k % NG + 1) * T], hps[:, :], ACT.Copy).then_inc(s_srow, 1)

            def exp_general(k):
                n, g = divmod(k, NG)
                if g < NG - 1:
                    return
                step = [0]

                def exp(tile):
                    step[0] += 1
                    act.wait_ge(s_garg[n], step[0])
                    nc.scalar.activation(tile, tile, ACT.Exp).then_inc(s_gexp[n], 1)

                with act.If(short[n] == 0):
                    for _ in range(NG):
                        exp(ab[:, :, :])
                    for _ in range(NG):
                        exp(ab[:, :, :])
                        exp(w3[:, :, :])
                with act.Else():
                    act.nop()

            def exp_prefix(k):
                n, g = divmod(k, NG)
                with act.If(short[n] != 0):
                    act.wait_ge(s_arg[n], g + 1)
                    nc.scalar.activation(ab[:, k % 2, :], ab[:, k % 2, :], ACT.Exp).then_inc(s_exp[n], 1)
                with act.Else():
                    act.nop()

            def scale_pooled(j):
                act.wait_ge(s_bkQ, j + 1)
                if j % GB == 0:
                    act.wait_ge(s_fac, j // GB + 1)
                if j >= OS:
                    act.wait_ge(s_store[j % OS], 16 * (j // OS))
                nc.scalar.activation(outs[:, j % OS, :], q_bank(j)[:, :], ACT.Copy, scale=fac[:, j:j + 1]).then_inc(s_pl, 1)

            scale_square(0)
            scale_square(1)
            scale_square(2)
            for k in range(GROUPS + 1):
                j = GB * (k - LAG)
                more = k < GROUPS
                if more:
                    keep_x1T(GB * k)
                if k == 0:
                    scale(3)
                elif k < GROUPS - 1:
                    scale_square(2 * k + 2)
                if more:
                    keep_x1T(GB * k + 1)
                if k == 0:
                    square(3)
                elif k < GROUPS - 1:
                    scale_square(2 * k + 3)
                if k >= 1:
                    tanh(k - 1)
                if more:
                    keep_x1T(GB * k + 2)
                if k >= 1:
                    keep_scores(k - 1)
                    if k == 1:
                        act.wait_ge(s_fast, 1)
                        short = [act.value_load(fasti[0:1, n:n + 1]) for n in range(NB)]
                    exp_general(k - 1)
                if k >= LAG:
                    scale_pooled(j)
                    scale_pooled(j + 1)
                if more:
                    keep_x1T(GB * k + 3)
                if k >= 1:
                    exp_prefix(k - 1)
                if k >= LAG:
                    scale_pooled(j + 2)
                    scale_pooled(j + 3)
            for j in range(GB * (GROUPS + 1 - LAG), TOT):
                scale_pooled(j)

        @block.gpsimd
        def _(pool):
            seq = [0]

            def link(ins):
                seq[0] += 1
                ins.then_inc(s_pool, 1)
                pool.wait_ge(s_pool, seq[0])

            def reflect(p):
                pool.wait_ge(s_xs, p + 1)
                w = xs[:, p % 2]
                pool.tensor_copy(w[:, :, 0:1], w[:, :, 2:3]).then_inc(s_pad, 1)
                pool.tensor_copy(w[:, :, D + 1:D + 2], w[:, :, D - 1:D]).then_inc(s_pad, 1)
                if pool_adds(p):
                    pool.wait_ge(s_pad, 2 * (p + 1))
                    if p >= 2:
                        pool.wait_ge(s_loc, p - 1)
                    add_shifted(pool, p)

            pool.memset(one[:, :], 1.0).then_inc(s_one, 1)
            link(pool.memset(ident[:, :], 0.0))
            link(pool.affine_select(out=ident[:, :], in_=ident[:, :], compare_op=ALU.not_equal, fill=1.0, base=0,
                                    pattern=[[-1, P]], channel_multiplier=1))
            link(pool.memset(offd, 0.0))
            for side in (1, -1):
                link(pool.affine_select(out=offd, in_=offd, compare_op=ALU.not_equal, fill=1.0, base=side,
                                        pattern=[[-1, P]], channel_multiplier=1))
            pool.nop().then_inc(s_con, 1)
            reflect(0)
            link(pool.iota(cnti[:, :], pattern=[[P, NBLK]], base=1, channel_multiplier=1))
            pool.tensor_copy(cnt[:, :], cnti[:, :]).then_inc(s_cnt, 1)
            for p in range(1, TOT // 2):
                reflect(p)

        @block.vector
        def _(dve):
            vec = nc.vector

            def chain(s):
                seq = [0]

                def link(ins):
                    seq[0] += 1
                    ins.then_inc(s, 1)
                    dve.wait_ge(s, seq[0])
                return link

            link = chain(s_dve)
            plink = [chain(s) for s in s_dp]
            glink = [chain(s) for s in s_dg]

            dve.wait_ge(s_small, 48)
            link(vec.tensor_tensor(cdia[:, :], z[:, 0, :], z[:, 1, :], ALU.add))
            link(vec.scalar_tensor_tensor(out=cdia[:, :], in0=cdia[:, :], scalar=-2.0, in1=z[:, 2, :], op0=ALU.mult, op1=ALU.add))
            link(vec.tensor_scalar(cdia[:, :], cdia[:, :], 1.0, None, ALU.add))
            link(vec.tensor_scalar(nzR[:, :], z[:, 2, :], -1.0, None, ALU.mult))
            dve.wait_ge(s_con, 1)

            def tridiagonal(n):
                link(vec.tensor_scalar(tri[:, n, :], ident[:, :], cdia[:, n:n + 1], None, ALU.mult))
                vec.scalar_tensor_tensor(out=tri[:, n, :], in0=offd, scalar=z[:, 1, n:n + 1], in1=tri[:, n, :],
                                         op0=ALU.mult, op1=ALU.add).then_inc(s_tri, 1)

            def left_right(p):
                dve.wait_ge(s_pad, 2 * (p + 1))
                if p >= 2:
                    dve.wait_ge(s_loc, p - 1)
                add_shifted(vec, p)

            def local(p):
                n = p // (NBLK // 2)
                dve.wait_ge(s_lr[p % 2], p // 2 + 1)
                dve.wait_ge(s_sq, p + 1)
                to = loc[:, p % LS, :, :]
                vec.scalar_tensor_tensor(out=to, in0=to, scalar=nzR[:, n:n + 1], in1=lr[:, p % 2, :, :],
                                         op0=ALU.mult, op1=ALU.add).then_inc(s_loc, 1)

            def borders(k):
                n, g = divmod(k, NG)
                dve.wait_ge(s_xT, GB * (k + 1))
                if k == 0:
                    dve.wait_ge(s_bT, NB)
                w = x1T[:, k % RS, :, :].rearrange("p c (b t) -> p c b t", b=GB)
                for side, col in ((0, 0), (TOT, P - 1)):
                    at = side + GB * k
                    edge = w[:, :, :, col:col + 1].rearrange("p c b t -> p c (b t)")
                    vec.tensor_tensor(edge, edge, bT[:, :, at:at + GB], ALU.add).then_inc(s_fix, 1)

            def constants():
                dve.wait_ge(s_w, 48)
                vec.tensor_scalar(vrep[:, :], ident[:, :], 0.0, vs[:, 0:1], ALU.mult, ALU.add).then_inc(s_vrep, 1)
                vec.scalar_tensor_tensor(out=vabs[:, :], in0=vs[:, :], scalar=-1.0, in1=vs[:, :], op0=ALU.mult, op1=ALU.max).then_inc(s_vrep, 1)

            def turned_borders():
                dve.wait_ge(s_bt, 1)
                border = lps[:, 0:DC * 2 * TOT].rearrange("p (c r) -> p c r", c=2 * DC)
                scaled = bT.rearrange("p c (s r) -> p (c s) r", s=2)
                for n in range(NB):
                    rows = slice(NBLK * n, NBLK * (n + 1))
                    vec.tensor_scalar(scaled[:, :, rows], border[:, :, rows], z[:, 1, n:n + 1], None, ALU.mult).then_inc(s_bT, 1)

            def flags():
                dve.wait_ge(s_ti, 16)
                dve.wait_ge(s_cnt, 1)
                link(vec.tensor_copy(tf[:, :], ti[:, :]))
                link(vec.tensor_scalar(t[:, 0, :], tf[:, :], 0.0, None, ALU.is_equal))
                link(vec.tensor_scalar(t[:, 1, :], tf[:, :], 1.0, None, ALU.is_equal))
                link(vec.tensor_tensor(t[:, 2, :], t[:, 0, :], t[:, 1, :], ALU.add))
                link(vec.tensor_scalar(t[:, 2, :], t[:, 2, :], -1.0, 1.0, ALU.mult, ALU.add))
                for k, flag in enumerate((1, 0, 2)):
                    link(vec.tensor_scalar(allow[:, k, :], t[:, flag, :], -1.0, 1.0, ALU.mult, ALU.add))
                link(vec.tensor_scalar(pen[:, :, :], allow[:, :, :], BIG, -BIG, ALU.mult, ALU.add))
                link(vec.tensor_tensor(cslope[:, :], t[:, 0, :], t[:, 1, :], ALU.subtract))
                link(vec.tensor_scalar(cbase[:, :], t[:, 1, :], float(S + 1), None, ALU.mult))
                link(vec.scalar_tensor_tensor(out=cbase[:, :], in0=t[:, 2, :], scalar=float(S - 1), in1=cbase[:, :],
                                              op0=ALU.mult, op1=ALU.add))
                dve.wait_ge(s_v1, 1)
                link(vec.tensor_scalar(fast[:, :], t[:, 0, :], 0.0, None, ALU.mult))
                link(vec.tensor_scalar(fast[:, :], fast[:, :], lps[:, 511:512], V_MAX, ALU.add, ALU.is_le))
                link(vec.tensor_tensor(fast[:, :], fast[:, :], t[:, 0, :], ALU.mult))
                vec.tensor_copy(fasti[:, :], fast[:, :]).then_inc(s_fast, 1)
                dve.wait_ge(s_fast, 1)

            def slot_free(k):
                if k >= RS:
                    dve.wait_ge(s_bkQ, GB * (k - RS + 1))

            def over_chunks(row):
                return row.rearrange("p (o t) -> p o t", o=1).to_broadcast([P, DC, T])

            def prefix_rho(k):
                n, g = divmod(k, NG)
                lk = plink[n]
                o = g * T
                dve.wait_ge(s_srow, k + 1)
                rho = ab[:, k % 2, :]
                if g == 0:
                    lk(vec.memset(rho[:, 0:1], 0.0))
                    vec.tensor_tensor(rho[:, 1:T], srow[:, 0:T - 1], srow[:, 1:T], ALU.subtract).then_inc(s_arg[n], 1)
                else:
                    vec.tensor_tensor(rho, srow[:, o - 1:o + T - 1], srow[:, o:o + T], ALU.subtract).then_inc(s_arg[n], 1)

            def prefix_L(k):
                n, g = divmod(k, NG)
                lk = plink[n]
                dve.wait_ge(s_exp[n], g + 1)
                if k >= 1:
                    dve.wait_ge(s_Lc, k)
                if g == 0:
                    dve.wait_ge(s_one, 1)
                    lk(vec.memset(L_r[:, 0:1], 0.0))
                else:
                    lk(vec.tensor_copy(L_r[:, 0:1], L_r[:, T:T + 1]))
                vec.tensor_tensor_scan(L_r[:, 1:T + 1], ab[:, k % 2, :], one[:, 0:1].to_broadcast([P, T]), L_r[:, 0:1],
                                       ALU.mult, ALU.add).then_inc(s_L, 1)

            def prefix_scan(k, outputs=()):
                n, g = divmod(k, NG)
                prefix_L(k)
                slot_free(k)
                dve.wait_ge(s_fix, 2 * (k + 1))
                for c in range(DC):
                    start = 0.0 if g == 0 else G[:, (k - 1) % RS, c, T - 1:T]
                    vec.tensor_tensor_scan(G[:, k % RS, c, :], ab[:, k % 2, :], x1T[:, k % RS, c, :], start,
                                           ALU.mult, ALU.add).then_inc(s_G, 1)
                    if outputs:
                        output(outputs[c])
                dve.wait_ge(s_L, k + 1)
                dve.wait_ge(s_G, DC * (k + 1))

            def prefix_factor(k):
                n, g = divmod(k, NG)
                lk = plink[n]
                f = fac[:, GB * k:GB * (k + 1)]
                dve.wait_ge(s_Lc, k + 1)
                lk(vec.tensor_tensor(f, lps[:, 0:GB], cnt[:, GB * g:GB * (g + 1)], ALU.mult))
                vec.reciprocal(f, f).then_inc(s_fac, 1)
                dve.wait_ge(s_fac, k + 1)

            def general(k):
                n = k // NG
                lk = glink[n]
                step = [0]

                def exp(ins):
                    step[0] += 1
                    ins.then_inc(s_garg[n], 1)
                    dve.wait_ge(s_gexp[n], step[0])

                dve.wait_ge(s_srow, k + 1)
                dve.wait_ge(s_one, 1)
                dve.wait_ge(s_fix, 2 * (k + 1))
                dve.wait_ge(s_Lc, k)
                slot_free(k)
                for col, val in ((mF[:, 0:1], -BIG), (mB[:, S:S + 1], -BIG), (LF[:, 0:1], 0.0), (LB[:, S:S + 1], 0.0)):
                    lk(vec.memset(col, val))
                unit = one[:, 0:1].to_broadcast([P, T])
                lk(vec.tensor_tensor_scan(mF[:, 1:S + 1], srow[:, :], srow[:, :], mF[:, 0:1], ALU.max, ALU.max))
                lk(vec.tensor_tensor_scan(mB[:, 0:S][:, ::-1], srow[:, ::-1], srow[:, ::-1], mB[:, S:S + 1], ALU.max, ALU.max))
                for g in range(NG):
                    o, slot = g * T, (NG * n + g) % RS
                    lk(vec.tensor_tensor(ab[:, 0, :], mF[:, o:o + T], mF[:, o + 1:o + T + 1], ALU.subtract))
                    exp(vec.tensor_tensor(ab[:, 1, :], srow[:, o:o + T], mF[:, o + 1:o + T + 1], ALU.subtract))
                    lk(vec.tensor_tensor_scan(LF[:, o + 1:o + T + 1], ab[:, 0, :], ab[:, 1, :], LF[:, o:o + 1], ALU.mult, ALU.add))
                    lk(vec.tensor_tensor(G[:, slot, :, :], x1T[:, slot, :, :], over_chunks(ab[:, 1, :]), ALU.mult))
                    for c in range(DC):
                        row = G[:, slot, c, :]
                        start = 0.0 if g == 0 else G[:, (NG * n + g - 1) % RS, c, T - 1:T]
                        lk(vec.tensor_tensor_scan(row, ab[:, 0, :], row, start, ALU.mult, ALU.add))
                for g in reversed(range(NG)):
                    o, slot = g * T, (NG * n + g) % RS
                    lk(vec.tensor_tensor(ab[:, 0, :], mB[:, o + 1:o + T + 1], mB[:, o:o + T], ALU.subtract))
                    exp(vec.tensor_tensor(ab[:, 1, :], srow[:, o:o + T], mB[:, o:o + T], ALU.subtract))
                    lk(vec.tensor_tensor_scan(LB[:, o:o + T][:, ::-1], ab[:, 0, ::-1], ab[:, 1, ::-1], LB[:, o + T:o + T + 1],
                                              ALU.mult, ALU.add))
                    src = (mF[:, o:o + T], mB[:, o + 1:o + T + 1], srow[:, o:o + T])
                    lk(vec.tensor_scalar(rden[:, :], src[0], pen[:, 0, n:n + 1], None, ALU.add))
                    for q in (1, 2):
                        lk(vec.scalar_tensor_tensor(out=rden[:, :], in0=src[q], scalar=pen[:, q, n:n + 1], in1=rden[:, :],
                                                    op0=ALU.add, op1=ALU.max))
                    for q in range(3):
                        lk(vec.tensor_tensor(w3[:, q, :], src[q], rden[:, :], ALU.subtract))
                    exp(vec.tensor_scalar(w3[:, :, :], w3[:, :, :], CLAMP, None, ALU.min))
                    for q in range(3):
                        lk(vec.tensor_scalar(w3[:, q, :], w3[:, q, :], allow[:, q, n:n + 1], None, ALU.mult))
                    lk(vec.tensor_tensor(dec[:, :], w3[:, 0, :], LF[:, o:o + T], ALU.mult))
                    lk(vec.tensor_tensor(wgt[:, :], w3[:, 1, :], LB[:, o + 1:o + T + 1], ALU.mult))
                    lk(vec.tensor_tensor(dec[:, :], dec[:, :], wgt[:, :], ALU.add))
                    lk(vec.tensor_tensor(dec[:, :], dec[:, :], w3[:, 2, :], ALU.add))
                    lk(vec.tensor_tensor_scan(rden[:, :], unit, unit, float(o), ALU.mult, ALU.add))
                    lk(vec.tensor_scalar(wgt[:, :], rden[:, :], cslope[:, n:n + 1], cbase[:, n:n + 1], ALU.mult, ALU.add))
                    lk(vec.tensor_tensor(dec[:, :], dec[:, :], wgt[:, :], ALU.mult))
                    lk(vec.reciprocal(rden[:, :], dec[:, :]))
                    for q in range(3):
                        lk(vec.tensor_tensor(w3[:, q, :], w3[:, q, :], rden[:, :], ALU.mult))
                    for c in range(DC):
                        row, x1row = G[:, slot, c, :], x1T[:, slot, c, :]
                        if g == NG - 1:
                            lk(vec.memset(back[:, T:T + 1], 0.0))
                        else:
                            lk(vec.tensor_copy(back[:, T:T + 1], carry[:, c:c + 1]))
                        lk(vec.tensor_tensor(back[:, 0:T], x1row, ab[:, 1, :], ALU.mult))
                        lk(vec.tensor_tensor_scan(back[:, 0:T][:, ::-1], ab[:, 0, ::-1], back[:, 0:T][:, ::-1], back[:, T:T + 1],
                                                  ALU.mult, ALU.add))
                        lk(vec.tensor_copy(carry[:, c:c + 1], back[:, 0:1]))
                        lk(vec.tensor_tensor(wgt[:, 1:T], w3[:, 0, 1:T], row[:, 0:T - 1], ALU.mult))
                        if g == 0:
                            lk(vec.memset(wgt[:, 0:1], 0.0))
                        else:
                            before = G[:, (NG * n + g - 1) % RS, c, T - 1:T]
                            lk(vec.tensor_tensor(wgt[:, 0:1], w3[:, 0, 0:1], before, ALU.mult))
                        lk(vec.tensor_tensor(dec[:, :], w3[:, 1, :], back[:, 1:T + 1], ALU.mult))
                        lk(vec.tensor_tensor(row, w3[:, 2, :], x1row, ALU.mult))
                        lk(vec.tensor_tensor(row, row, wgt[:, :], ALU.add))
                        lk(vec.tensor_tensor(row, row, dec[:, :], ALU.add))
                vec.memset(carry[:, 0:1], 0.0).then_inc(s_G, NG * DC)
                dve.wait_ge(s_G, DC * (k + 1))

            def branch(*steps):
                n = steps[0][0] // NG
                same = [step for step in steps if step[0] // NG == n]
                with dve.If(short[n] != 0):
                    for k, short_path, _ in same:
                        short_path(k)
                with dve.Else():
                    for k, _, other in same:
                        other(k)
                if len(same) < len(steps):
                    branch(*steps[len(same):])

            def no_L(k, outputs=()):
                if k >= 1:
                    dve.wait_ge(s_Lc, k)
                vec.memset(L_r[0:1, :], 1.0).then_inc(s_L, 1)
                dve.wait_ge(s_L, k + 1)
                for j in outputs:
                    output(j)

            def scan_general(k):
                if k % NG == NG - 1:
                    general(k)
                else:
                    dve.nop()

            def one_factor(k):
                dve.wait_ge(s_Lc, k + 1)
                vec.memset(fac[:, GB * k:GB * (k + 1)], 1.0).then_inc(s_fac, 1)

            def output(j):
                dve.wait_ge(s_pl, j + 1)
                dve.wait_ge(s_bkx, j + 1)
                vec.tensor_tensor(outs[:, j % OS, :], outs[:, j % OS, :], x1_bank(j)[:, :], ALU.add).then_inc(s_o, 1)

            tridiagonal(0)
            left_right(0)
            local(0)
            left_right(1)
            local(1)
            for k in range(GROUPS + 1):
                j = GB * (k - LAG)
                if k >= 2:
                    branch((k - 2, prefix_scan, no_L))
                if k + 1 < GROUPS:
                    left_right(2 * k + 2)
                    local(2 * k + 2)
                    if k == 0:
                        left_right(3)
                        local(3)
                        turned_borders()
                        constants()
                    if k == 1:
                        flags()
                        short = [dve.value_load(fasti[0:1, n:n + 1]) for n in range(NB)]
                if k >= 2:
                    branch((k - 2, prefix_factor, one_factor), (k - 1, prefix_rho, scan_general))
                elif k == 1:
                    branch((0, prefix_rho, scan_general))
                if k >= LAG:
                    output(j)
                    output(j + 1)
                if 1 <= k < GROUPS - 1:
                    local(2 * k + 3)
                if k < GROUPS:
                    borders(k)
                if k == 1:
                    for n in range(1, NB):
                        tridiagonal(n)
                    dve.wait_ge(s_tri, NB)
                if k >= LAG:
                    output(j + 2)
                    output(j + 3)
            j = TAIL + GB
            branch((GROUPS - 1, lambda k: prefix_scan(k, range(j, j + DC)), lambda k: no_L(k, range(j, j + DC))))
            for j in range(TAIL + GB + DC, TOT):
                if j == TOT - GB - 2:
                    branch((GROUPS - 1, prefix_factor, one_factor))
                output(j)

        @block.tensor
        def _(pe):
            mm = nc.tensor.matmul

            def stencil(i):
                n = i // NBLK
                p = i // 2
                ps = xps[i % XP]
                x_there(pe, p)
                pe.wait_ge(s_tri, n + 1)
                pe.wait_ge(s_loc, p + 1)
                if i >= XP:
                    pe.wait_ge(s_xT, i - XP + 1)
                for c in range(DC):
                    to = ps[:, c * P:(c + 1) * P]
                    mm(to, xin[:, p % XS, i % 2, c * P:(c + 1) * P], tri[:, n, :], start=True, stop=False)
                    last = mm(to, loc[:, p % LS, i % 2, c * P:(c + 1) * P], ident[:, :], is_transpose=True, start=False, stop=True)
                last.then_inc(s_A, 1)

            def w1_product(k):
                pe.wait_ge(s_fix, 2 * (k + 1))
                if k >= 1:
                    pe.wait_ge(s_srow, k)
                else:
                    pe.wait_ge(s_w, 48)
                for c in range(DC):
                    last = mm(hps[:, :], W1s[:, c, :], x1T[:, k % RS, c, :], start=(c == 0), stop=(c == DC - 1))
                last.then_inc(s_h, 1)

            def scores(k):
                pe.wait_ge(s_hT, k + 1)
                mm(hps[:, :], vrep[:, :], hT[:, :], start=True, stop=True).then_inc(s_s, 1)

            def turn_L(k):
                pe.wait_ge(s_L, k + 1)
                if k >= 1:
                    pe.wait_ge(s_fac, k)
                else:
                    pe.wait_ge(s_fast, 1)
                for b in range(GB):
                    last = nc.tensor.transpose(lps[:, b:b + 1], L_r[0:1, 1 + b * P:1 + (b + 1) * P], ident[0:1, 0:1])
                last.then_inc(s_Lc, 1)

            def back_x1(j):
                k, b = divmod(j, GB)
                if j >= TAIL + 4:
                    pe.wait_ge(s_o, j - 3)
                elif j >= TAIL + 2:
                    pe.wait_ge(s_xT, TOT)
                elif j >= 2:
                    pe.wait_ge(s_o, j - 1)
                for c in range(DC):
                    last = nc.tensor.transpose(x1_bank(j)[:, c * P:(c + 1) * P], x1T[:, k % RS, c, b * P:(b + 1) * P], ident[:, :])
                last.then_inc(s_bkx, 1)

            def back_Q(j):
                k, b = divmod(j, GB)
                pe.wait_ge(s_G, DC * (k + 1))
                if j >= TAIL + 3:
                    pe.wait_ge(s_pl, j - 2)
                elif j == TAIL + 2:
                    pe.wait_ge(s_srow, GROUPS)
                elif j >= 2:
                    pe.wait_ge(s_pl, j - 1)
                for c in range(DC):
                    last = nc.tensor.transpose(q_bank(j)[:, c * P:(c + 1) * P], G[:, k % RS, c, b * P:(b + 1) * P], ident[:, :])
                last.then_inc(s_bkQ, 1)

            pe.wait_ge(s_con, 1)
            for _ in range(WARM):
                mm(hps[:, 0:P], ident[:, :], ident[:, :], start=True, stop=True)
            for k in range(GROUPS):
                j = GB * (k - LAG)
                stencil(GB * k)
                stencil(GB * k + 1)
                if k == 1:
                    pe.wait_ge(s_vrep, 2)
                    pe.wait_ge(s_one, 1)
                    pe.wait_ge(s_bT, NB)
                    mm(lps[:, 511:512], one[:, 0:1].to_broadcast([A, P]), vabs[:, :], start=True, stop=True).then_inc(s_v1, 1)
                if k >= LAG:
                    back_x1(j)
                if k >= 1:
                    w1_product(k - 1)
                if k >= LAG:
                    back_x1(j + 1)
                if k >= 2:
                    turn_L(k - 2)
                stencil(GB * k + 2)
                if k >= 1:
                    scores(k - 1)
                if k >= LAG:
                    back_Q(j)
                    back_Q(j + 1)
                if k == 0:
                    pe.wait_ge(s_brow, 32 * (NB + 1))
                    for c in range(DC):
                        last = nc.tensor.transpose(lps[:, c * 2 * TOT:(c + 1) * 2 * TOT], brow[:, c * P:(c + 1) * P],
                                                   ident[0:2 * TOT, 0:2 * TOT])
                    last.then_inc(s_bt, 1)
                stencil(GB * k + 3)
                if k >= LAG:
                    back_x1(j + 2)
                    back_Q(j + 2)
                    back_x1(j + 3)
                    back_Q(j + 3)
            w1_product(GROUPS - 1)
            turn_L(GROUPS - 2)
            back_x1(TAIL)
            back_x1(TAIL + 1)
            back_x1(TAIL + 2)
            scores(GROUPS - 1)
            back_Q(TAIL)
            back_Q(TAIL + 1)
            back_Q(TAIL + 2)
            for j in range(TAIL + 3, TOT):
                if j == TOT - GB - 3:
                    turn_L(GROUPS - 1)
                back_Q(j)
                back_x1(j)


_INS = ["x", "condB_zX", "condB_zY", "condB_zR", "itok_B_0_2", "L1_cond_W1", "L1_cond_b1", "L1_cond_v"]


def kernel(**inputs):
    import numpy as np
    import concourse.bacc as bacc
    from concourse.bass_utils import run_bass_kernel_spmd

    nc = bacc.Bacc("TRN2", target_bir_lowering=False, num_devices=1)
    arrays, args = {}, []
    for name in _INS:
        a = np.ascontiguousarray(inputs[name])
        arrays[f"in_{name}"] = a
        args.append(nc.dram_tensor(f"in_{name}", a.shape, mybir.dt.from_np(a.dtype), kind="ExternalInput").ap())
    out = nc.dram_tensor("out", (NB, S, D), mybir.dt.float32, kind="ExternalOutput").ap()
    build(nc, *args, out)
    r = run_bass_kernel_spmd(nc, [arrays], core_ids=[0])
    return r.results[0]["out"]
```
